# Optimizing a Trainium2 kernel written in Bass

```python
import numpy as np
import jax
import jax.numpy as jnp

def _softmax(x, axis=-1):
    return jax.nn.softmax(x, axis=axis)

def _gelu(x):
    return jax.nn.gelu(x, approximate=True)

def _silu(x):
    return jax.nn.silu(x)

def _sigmoid(x):
    return jax.nn.sigmoid(x)

def _layernorm(x, axis=-1, eps=1e-05):
    m = jnp.mean(x, axis=axis, keepdims=True)
    v = jnp.var(x, axis=axis, keepdims=True)
    return (x - m) / jnp.sqrt(v + eps)

def _scatter_add(tgt, idx, src, axis=0):
    return tgt.at[idx].add(src)

def _segment_sum(src, seg, n):
    return jax.ops.segment_sum(src, seg, n)
kernel_name = 'mk_xattn_ffn_d1_seqx_r8_0f091e'

def setup_inputs(seed: int=0):
    np.random.seed(seed)
    _w = jnp.asarray

    def _rec_inputs():
        import jax
        import jax.numpy as jnp
        _rk = jax.random.key(seed)
        x = 0.0002417 + 0.9998 * jax.random.normal(jax.random.fold_in(_rk, 1), (2, 512, 128), jnp.float32)
        _lenS = 512 - jax.random.randint(jax.random.fold_in(_rk, 7), (2,), 0, max(1, 512 // 4) + 1, jnp.int32)
        _lenS2 = 77 - jax.random.randint(jax.random.fold_in(_rk, 8), (2,), 0, max(1, 77 // 4) + 1, jnp.int32)
        _ctx_1024P = jax.random.normal(jax.random.fold_in(_rk, 11), (2, 16, 128), jnp.float32)
        _ctx_1024c = jax.random.dirichlet(jax.random.fold_in(_rk, 511), 0.3 * jnp.ones((16,), jnp.float32), (2, 77))
        _ctx_1024t = jnp.einsum('bsk,bkd->bsd', _ctx_1024c, _ctx_1024P)
        _ctx_1024t = _ctx_1024t * jax.lax.rsqrt(jnp.mean(jnp.square(_ctx_1024t)) + 1e-12) * 0.953939
        ctx_1024 = 7.22013e-05 + 1.00017 * (_ctx_1024t + 0.3 * jax.random.normal(jax.random.fold_in(_rk, 611), (2, 77, 128), jnp.float32))
        _validS = jnp.arange(512)[None, :] < _lenS[:, None]
        _validS2 = jnp.arange(77)[None, :] < _lenS2[:, None]
        _causal = jnp.tril(jnp.ones((512, 512), dtype=bool))
        mask_Bx1xSxS2_ik1 = jnp.where(jnp.broadcast_to(_validS2[:, None, None, :], (2, 1, 512, 77)), 1, 0).astype(jnp.int32)
        return (x, ctx_1024, mask_Bx1xSxS2_ik1)
    x, ctx_1024, mask_Bx1xSxS2_ik1 = _rec_inputs()

    def _L0_xattn_setup():
        import jax, jax.numpy as jnp
        import numpy as np
        EMBED = 128
        HEADS = 16
        HEAD_DIM = EMBED // HEADS
        B, S = (4, 256)
        key = jax.random.key(seed)
        ks = jax.random.split(key, 9)
        inp = {'values': jax.random.normal(ks[0], (B, S, EMBED), jnp.float32), 'keys': jax.random.normal(ks[1], (B, S, EMBED), jnp.float32), 'queries': jax.random.normal(ks[2], (B, S, EMBED), jnp.float32), 'mask': jax.random.randint(ks[3], (B, 1, S, S), 0, 2, jnp.int32), 'Wv': jax.random.normal(ks[4], (HEAD_DIM, HEAD_DIM), jnp.float32) / np.sqrt(HEAD_DIM), 'Wk': jax.random.normal(ks[5], (HEAD_DIM, HEAD_DIM), jnp.float32) / np.sqrt(HEAD_DIM), 'Wq': jax.random.normal(ks[6], (HEAD_DIM, HEAD_DIM), jnp.float32) / np.sqrt(HEAD_DIM), 'Wo': jax.random.normal(ks[7], (EMBED, EMBED), jnp.float32) / np.sqrt(EMBED), 'bo': jax.random.normal(ks[8], (EMBED,), jnp.float32) * 0.01}
        return inp
    _L0_xattn_all = _L0_xattn_setup()
    _L0_xattn_in = {k: v for k, v in _L0_xattn_all.items() if k in ('Wv', 'Wk', 'Wq', 'Wo', 'bo')}
    del _L0_xattn_all

    def _L0_ffn_setup():
        import jax, jax.numpy as jnp
        import numpy as np
        TOP_K = 2

        def _mlp(x, w_fc, w_proj):
            return jnp.square(jax.nn.relu(x @ w_fc.T)) @ w_proj.T
        key = jax.random.key(seed)
        ks = jax.random.split(key, 6)
        B, S, D, E = (4, 256, 128, 8)
        d_ff = 4 * D
        x = jax.random.normal(ks[0], (B, S, D), dtype=jnp.float32)
        router_w = jax.random.normal(ks[1], (E, D), dtype=jnp.float32) * 0.02
        w_fc = jax.random.normal(ks[2], (E, d_ff, D), dtype=jnp.float32) * 0.02
        w_proj = jax.random.normal(ks[3], (E, D, d_ff), dtype=jnp.float32) * 0.02
        shared_fc = jax.random.normal(ks[4], (d_ff, D), dtype=jnp.float32) * 0.02
        shared_proj = jax.random.normal(ks[5], (D, d_ff), dtype=jnp.float32) * 0.02
        return {'x': x, 'router_w': router_w, 'w_fc': w_fc, 'w_proj': w_proj, 'shared_fc': shared_fc, 'shared_proj': shared_proj}
    _L0_ffn_all = _L0_ffn_setup()
    _L0_ffn_in = {k: v for k, v in _L0_ffn_all.items() if k in ('router_w', 'w_fc', 'w_proj', 'shared_fc', 'shared_proj')}
    del _L0_ffn_all
    return {'x': x, 'ctx_1024': ctx_1024, 'mask_Bx1xSxS2_ik1': mask_Bx1xSxS2_ik1, 'L0_xattn_Wv': _L0_xattn_in['Wv'], 'L0_xattn_Wk': _L0_xattn_in['Wk'], 'L0_xattn_Wq': _L0_xattn_in['Wq'], 'L0_xattn_Wo': _L0_xattn_in['Wo'], 'L0_xattn_bo': _L0_xattn_in['bo'], 'L0_ffn_router_w': _L0_ffn_in['router_w'], 'L0_ffn_w_fc': _L0_ffn_in['w_fc'], 'L0_ffn_w_proj': _L0_ffn_in['w_proj'], 'L0_ffn_shared_fc': _L0_ffn_in['shared_fc'], 'L0_ffn_shared_proj': _L0_ffn_in['shared_proj']}

def reference(x, ctx_1024, mask_Bx1xSxS2_ik1, L0_xattn_Wv, L0_xattn_Wk, L0_xattn_Wq, L0_xattn_Wo, L0_xattn_bo, L0_ffn_router_w, L0_ffn_w_fc, L0_ffn_w_proj, L0_ffn_shared_fc, L0_ffn_shared_proj):
    import jax
    import jax.numpy as jnp

    def _L0_xattn_ref(values, keys, queries, mask, Wv, Wk, Wq, Wo, bo):
        import jax, jax.numpy as jnp
        import numpy as np
        EMBED = 128
        HEADS = 16
        HEAD_DIM = EMBED // HEADS
        B, S = (4, 256)
        N, q_len = (queries.shape[0], queries.shape[1])
        v_len, k_len = (values.shape[1], keys.shape[1])
        v = values.reshape(N, v_len, HEADS, HEAD_DIM)
        k = keys.reshape(N, k_len, HEADS, HEAD_DIM)
        q = queries.reshape(N, q_len, HEADS, HEAD_DIM)
        v = jnp.einsum('nlhd,ed->nlhe', v, Wv)
        k = jnp.einsum('nlhd,ed->nlhe', k, Wk)
        q = jnp.einsum('nlhd,ed->nlhe', q, Wq)
        energy = jnp.einsum('nqhd,nkhd->nhqk', q, k)
        energy = jnp.where(mask == 0, jnp.float32(-1e+20), energy)
        attention = jax.nn.softmax(energy / np.sqrt(EMBED).astype(np.float32), axis=3)
        out = jnp.einsum('nhql,nlhd->nqhd', attention, v).reshape(N, q_len, EMBED)
        return out @ Wo.T + bo

    def _L0_ffn_ref(x, router_w, w_fc, w_proj, shared_fc, shared_proj):
        import jax, jax.numpy as jnp
        import numpy as np
        TOP_K = 2

        def _mlp(x, w_fc, w_proj):
            return jnp.square(jax.nn.relu(x @ w_fc.T)) @ w_proj.T
        B, S, D = x.shape
        E = router_w.shape[0]
        T = B * S
        flat = x.reshape(T, D)
        logits = flat @ router_w.T
        probs = jax.nn.softmax(logits.astype(jnp.float32), axis=-1)
        topk_p, topk_i = jax.lax.top_k(probs, TOP_K)
        topk_w = (topk_p / jnp.maximum(topk_p.sum(-1, keepdims=True), 1e-09)).astype(flat.dtype)
        combine = jnp.zeros((T, E), dtype=flat.dtype)
        combine = combine.at[jnp.arange(T)[:, None], topk_i].add(topk_w)
        out = jnp.zeros_like(flat)
        for e in range(E):
            out = out + _mlp(flat, w_fc[e], w_proj[e]) * combine[:, e:e + 1]
        out = out + _mlp(flat, shared_fc, shared_proj)
        return out.reshape(B, S, D)
    x = x + _L0_xattn_ref(ctx_1024, ctx_1024, _layernorm(x, axis=-1), mask_Bx1xSxS2_ik1, L0_xattn_Wv, L0_xattn_Wk, L0_xattn_Wq, L0_xattn_Wo, L0_xattn_bo)
    x = x + _L0_ffn_ref(_layernorm(x, axis=-1), L0_ffn_router_w, L0_ffn_w_fc, L0_ffn_w_proj, L0_ffn_shared_fc, L0_ffn_shared_proj)
    return x

_drawn_inputs = setup_inputs


def setup_inputs(seed=0):
    import zlib

    import numpy as np

    out = dict(_drawn_inputs(seed))
    spreads = {}
    factors = {'L0_xattn_bo': 5.91,
     'L0_ffn_router_w': 3.577,
     'L0_ffn_w_fc': 3.433,
     'L0_ffn_w_proj': 3.087,
     'L0_ffn_shared_fc': 2.922}
    for name, (base, spread) in spreads.items():
        noise = np.random.default_rng([zlib.crc32(name.encode()), seed]).standard_normal(out[name].shape)
        drawn = base * np.exp(spread * noise) if base else spread * noise
        out[name] = jnp.asarray(drawn.astype(out[name].dtype))
    for name, factor in factors.items():
        out[name] = (out[name] * factor).astype(out[name].dtype)
    return out
```

```python
from contextlib import ExitStack

import concourse.bass as bass
from concourse import mybir

F32 = mybir.dt.float32
F32R = mybir.dt.float32r
BF16 = mybir.dt.bfloat16
I32 = mybir.dt.int32
ALU = mybir.AluOpType
ACT = mybir.ActivationFunctionType
AX_X = mybir.AxisListType.X

P = 128
B, S, D = 2, 512, 128
NT = B * S // P
TB = S // P
H, HD = 16, 8
SK = 77
SKP = 80
UH = H // 2
JH = 4
NU = NT * 2
UPB = TB * 2
CH = UH * SKP // P
NE = 8
NN = NE + 1
FF = 512
FT = FF // P
BPN = B * FT
NB = NN * BPN
LAG = 2
EPS = 1e-5
MASKED = -1e20
SCALE = 1.0 / float(D) ** 0.5
SMALL = 3 * HD


def xattn_moe(nc, x, ctx_t, mask, small, wo_r, bo, w_all, out):
    ctx = ExitStack()
    with ctx:
        def sb(name, shape, dt):
            return ctx.enter_context(nc.sbuf_tensor(name, shape, dt))

        def sem(name):
            return ctx.enter_context(nc.semaphore(name))

        root_dram = nc.dram_tensor("root_dram", (NE, B * S), F32).ap()

        x_sb = sb("x_sb", [P, NT, D], F32)
        ctx_sb = sb("ctx_sb", [P, B * SK], F32)
        mask_sb = sb("mask_sb", [P, NT, SK], I32)
        small_sb = sb("small_sb", [P, SMALL], F32)
        wo_sb = sb("wo_sb", [P, D + NE], F32)
        bo_sb = sb("bo_sb", [P, D], F32)
        ident = sb("ident", [P, P], F32)
        ident_bf = sb("ident_bf", [P, P], BF16)
        head_mask = sb("head_mask", [P, H], F32)
        group_mask = sb("group_mask", [P, JH], F32)
        minus_half = sb("minus_half", [P, TB], F32)
        plus_half = sb("plus_half", [P, TB * NE], F32)
        prio = sb("prio", [P, NE], F32)
        stats = sb("stats", [P, 2, NT, 6], F32)
        mv = sb("mv", [P, 2, NT, 2], F32)
        var_eps = sb("var_eps", [P, 2, NT], F32)
        rstd = sb("rstd", [P, 2, NT], F32)
        xn = sb("xn", [P, NT, D], F32)
        xn_hi = sb("xn_hi", [P, B, S], F32R)
        xn_lo = sb("xn_lo", [P, B, S], F32R)
        bd = sb("bd", [P, 3, H, HD], F32)
        k_t = sb("k_t", [P, B * SK], F32)
        v_t = sb("v_t", [P, B, SK], F32)
        kblk = sb("kblk", [P, B, JH, SK], F32)
        kblk_hi = sb("kblk_hi", [P, B, JH, SK], F32R)
        kblk_lo = sb("kblk_lo", [P, B, JH, SK], F32R)
        vblk_t = sb("vblk_t", [P, B, H, SKP], F32)
        vblk = sb("vblk", [P, B * 2 * CH, P], F32)
        mask_bias = sb("mask_bias", [P, NT, SK], BF16)
        s_max = sb("s_max", [P, 2, UH], F32)
        s_sum = sb("s_sum", [P, 2, UH], F32)
        s_rec = sb("s_rec", [P, 2, UH], F32)
        s_sub = sb("s_sub", [P, 2, UH, SK], F32)
        prob = sb("prob", [P, 2, UH, SK], F32)
        prob_n = sb("prob_n", [P, 2, UH, SKP], F32)
        prob_t = sb("prob_t", [P, 2, CH, S], F32)
        attn_t = sb("attn_t", [P, S], F32)
        x_bo = sb("x_bo", [P, NT, D], F32)
        x2 = sb("x2", [P, NT, D], F32)
        xn2 = sb("xn2", [P, NT, D], F32)
        xn2_t = sb("xn2_t", [P, B, S], F32)
        x2_hi = sb("x2_hi", [P, B, S], F32R)
        x2_lo = sb("x2_lo", [P, B, S], F32R)
        r_exp = sb("r_exp", [P, B, TB, NE], F32)
        r_p = sb("r_p", [P, TB, NE], F32)
        r_a = sb("r_a", [P, TB, NE], F32)
        r_b = sb("r_b", [P, TB, NE], F32)
        r_c = sb("r_c", [P, TB, NE], F32)
        r_s = sb("r_s", [P, 8, TB], F32)
        comb = sb("comb", [P, B, TB, NE], F32)
        root = sb("root", [P, B, TB, NE], F32)
        root_t = sb("root_t", [TB * NE, B, P], F32)
        w_raw = sb("w_raw", [P, 2, 2 * FF], F32)
        w_hi = sb("w_hi", [P, 2, 2 * FF], F32R)
        w_lo = sb("w_lo", [P, 2, 2 * FF], F32R)
        root_b = sb("root_b", [P, 2, B, S], F32)
        xs = sb("xs", [P, B, S], F32)
        xs_hi = sb("xs_hi", [P, B, S], F32R)
        xs_lo = sb("xs_lo", [P, B, S], F32R)
        hid_r = sb("hid_r", [P, 2, S], F32)
        hid = sb("hid", [P, 2, S], F32)
        hid_hi = sb("hid_hi", [P, FT, S], F32R)
        hid_lo = sb("hid_lo", [P, FT, S], F32R)
        y_t = sb("y_t", [P, B, S], F32)
        y_out = sb("y_out", [P, NT, D], F32)

        ps = ctx.enter_context(nc.psum_tensor("ps", [P, 8, 512], F32))
        PROB_BANK = (4, 5)
        Y_BANK = (4, 5)
        PV_BANK, MISC_BANK = 6, 7

        x_in = [sem("x_in0"), sem("x_in1")]
        ctx_in, mask_in, small_in, wo_in, bo_in = (sem(n) for n in (
            "ctx_in", "mask_in", "small_in", "wo_in", "bo_in"))
        w_in = [sem("w_in0"), sem("w_in1")]
        root_in = [[sem(f"root_in{q}{h}") for h in range(B)] for q in range(2)]
        root_out = [sem("root_out0"), sem("root_out1")]
        out_done = sem("out_done")
        pool_step, dve_step = sem("pool_step"), sem("dve_step")
        ident_ready, const_ready, bd_ready, group_ready = (sem(n) for n in (
            "ident_ready", "const_ready", "bd_ready", "group_ready"))
        bias_ready, xbo_ready, vblk_t_ready = sem("bias_ready"), sem("xbo_ready"), sem("vblk_t_ready")
        var_ready, rstd_ready, xn_ready = sem("var_ready"), sem("rstd_ready"), sem("xn_ready")
        xt_done, xn_hi_done, xn_lo_done = sem("xt_done"), sem("xn_hi_done"), sem("xn_lo_done")
        kv_done, kv_read, kq_done, kblk_ready = (sem(n) for n in (
            "kv_done", "kv_read", "kq_done", "kblk_ready"))
        vt_done, vblk_ready = sem("vt_done"), sem("vblk_ready")
        score_done, max_done, sub_done, exp_done, sum_done, rec_done, norm_done = (sem(n) for n in (
            "score_done", "max_done", "sub_done", "exp_done", "sum_done", "rec_done", "norm_done"))
        pt_done, pt_read, pv_half, attn_read, proj_o = (sem(n) for n in (
            "pt_done", "pt_read", "pv_half", "attn_read", "proj_o"))
        x2_done, xt2_done, xn2_read, x2_hi_done, x2_lo_done = (sem(n) for n in (
            "x2_done", "xt2_done", "xn2_read", "x2_hi_done", "x2_lo_done"))
        logit_done, logit_read, rexp_done, comb_done, root_done, root_t_done, root_t_read = (
            sem(n) for n in ("logit_done", "logit_read", "rexp_done", "comb_done", "root_done",
                             "root_t_done", "root_t_read"))
        w_hi_done, w_lo_done = sem("w_hi_done"), sem("w_lo_done")
        xs_done, xs_hi_done, xs_lo_done = sem("xs_done"), sem("xs_hi_done"), sem("xs_lo_done")
        up_done, relu_done, square_done, hid_hi_done, hid_lo_done, down_done = (sem(n) for n in (
            "up_done", "relu_done", "square_done", "hid_hi_done", "hid_lo_done", "down_done"))
        y_read, y_t_done, y_ready = sem("y_read"), sem("y_t_done"), sem("y_ready")

        def at_least(eng, s, n):
            if not isinstance(n, int) or n > 0:
                eng.wait_ge(s, n)

        def heads_of(bank):
            return ps[:, bank, 0:JH * SK].rearrange("p (j k) -> p j k", k=SK)

        def slot_of(n):
            return (n + 1) % 2

        block = ctx.enter_context(nc.Block())

        @block.sync
        def _(sp):
            x_v = x.rearrange("(t p) d -> p t d", p=P)
            sp.dma_start(x_sb[:, 0:TB, :], x_v[:, 0:TB, :]).then_inc(x_in[0], 16)
            sp.dma_start(mask_sb[:, :, :], mask.rearrange("(t p) k -> p t k", p=P)).then_inc(mask_in, 16)
            sp.dma_start(x_sb[:, TB:NT, :], x_v[:, TB:NT, :]).then_inc(x_in[1], 16)
            sp.dma_start(wo_sb[:, :], wo_r).then_inc(wo_in, 16)
            sp.dma_start(bo_sb[:, :], bo.partition_broadcast(P)).then_inc(bo_in, 16)
            for n in range(2):
                sp.dma_start(w_raw[:, slot_of(n), :], w_all[n, :, :]).then_inc(w_in[slot_of(n)], 16)

            def load_w(n, slot):
                at_least(sp, w_lo_done, n - 1)
                sp.dma_start(w_raw[:, slot, :], w_all[n, :, :]).then_inc(w_in[slot], 16)

            def load_root(n, slot, h):
                at_least(sp, xs_done, 2 * (n - 1) + h - 3)
                sp.dma_start(root_b[:, slot, h, :],
                             root_dram[n - 1, h * S:(h + 1) * S].partition_broadcast(P))\
                  .then_inc(root_in[slot][h], 16)

            load_w(2, 1)
            for h in range(B):
                sp.wait_ge(root_t_read, h + 1)
                sp.dma_start(root_dram.rearrange("e (b t p) -> b t e p", b=B, t=TB)[h, :, :, :],
                             root_t[:, h, :]).then_inc(root_out[h], 16)
                sp.wait_ge(root_out[h], 16)
                load_root(1, 0, h)
                load_root(2, 1, h)
            for n in range(3, NN):
                load_w(n, slot_of(n))
                for h in range(B):
                    load_root(n, slot_of(n), h)
            out_v = out.rearrange("(t p) d -> p t d", p=P)
            for h in range(B):
                sp.wait_ge(y_ready, h + 1)
                sp.dma_start(out_v[:, h * TB:(h + 1) * TB, :], y_out[:, h * TB:(h + 1) * TB, :])\
                  .then_inc(out_done, 16)
            sp.wait_ge(out_done, 16 * B)

        @block.gpsimd
        def _(pool):
            steps = [0]

            def link(ins):
                steps[0] += 1
                ins.then_inc(pool_step, 1)
                pool.wait_ge(pool_step, steps[0])

            link(pool.memset(ident[:, :], 0.0))
            link(pool.affine_select(out=ident[:, :], in_=ident[:, :], compare_op=ALU.not_equal, fill=1.0,
                                    base=0, pattern=[[-1, P]], channel_multiplier=1))
            pool.tensor_copy(ident_bf[:, :], ident[:, :]).then_inc(ident_ready, 1)
            link(pool.memset(minus_half[:, :], -0.5))
            link(pool.memset(head_mask[:, :], 1.0))
            link(pool.affine_select(out=head_mask[:, :], in_=head_mask[:, :], compare_op=ALU.is_ge, fill=0.0,
                                    base=0, pattern=[[-HD, H]], channel_multiplier=1))
            link(pool.affine_select(out=head_mask[:, :], in_=head_mask[:, :], compare_op=ALU.is_ge, fill=0.0,
                                    base=HD - 1, pattern=[[HD, H]], channel_multiplier=-1))
            pool.wait_ge(small_in, 16)
            for i in range(3):
                pool.tensor_tensor(bd[:, i, :, :],
                                   small_sb[:, i * HD:(i + 1) * HD].unsqueeze(1).broadcast_to([P, H, HD]),
                                   head_mask[:, :].unsqueeze(2).broadcast_to([P, H, HD]),
                                   ALU.mult).then_inc(bd_ready, 1)

            def root_inverse(i, which, g):
                pool.wait_ge(var_ready, i + 1)
                pool.tensor_tensor(rstd[:, which, g * TB:(g + 1) * TB], var_eps[:, which, g * TB:(g + 1) * TB],
                                   minus_half[:, :], ALU.pow).then_inc(rstd_ready, 1)

            root_inverse(0, 0, 0)
            pool.wait_ge(mask_in, 16)
            pool.tensor_scalar(mask_bias[:, :, :], mask_sb[:, :, :], 0.0, MASKED, ALU.is_equal, ALU.mult)\
                .then_inc(bias_ready, 1)
            root_inverse(1, 0, 1)
            for i in range(NE):
                last = pool.memset(prio[:, i:i + 1], float(NE - i))
            last.then_inc(const_ready, 1)
            pool.memset(vblk_t[:, :, :, SK:SKP], 0.0).then_inc(const_ready, 1)
            pool.memset(prob_n[:, :, :, SK:SKP], 0.0).then_inc(const_ready, 1)

            def normalise(k):
                pool.wait_ge(rec_done, k + 1)
                at_least(pool, pt_done, 2 * (k - 1))
                pool.tensor_tensor(prob_n[:, k % 2, :, 0:SK], prob[:, k % 2, :, :],
                                   s_rec[:, k % 2, :].unsqueeze(2).broadcast_to([P, UH, SK]),
                                   ALU.mult).then_inc(norm_done, 1)

            def v_blocks(b):
                pool.wait_ge(kv_read, 2)
                pool.tensor_tensor(vblk_t[:, b, :, 0:SK], v_t[:, b, :].unsqueeze(1).broadcast_to([P, H, SK]),
                                   head_mask[:, :].unsqueeze(2).broadcast_to([P, H, SK]),
                                   ALU.mult).then_inc(vblk_t_ready, 1)

            def split_lo(n, slot):
                pool.wait_ge(w_hi_done, n + 1)
                pool.tensor_tensor(w_lo[:, slot, :], w_raw[:, slot, :], w_hi[:, slot, :].bitcast(F32),
                                   ALU.subtract).then_inc(w_lo_done, 1)

            for k in range(NU):
                normalise(k)
                if k in (0, 2):
                    v_blocks(k // 2)
                if k == 4:
                    pool.wait_ge(bo_in, 16)
                    pool.wait_ge(x_in[0], 16)
                    pool.wait_ge(x_in[1], 16)
                    pool.tensor_tensor(x_bo[:, :, :], x_sb[:, :, :],
                                       bo_sb[:, :].unsqueeze(1).broadcast_to([P, NT, D]), ALU.add)\
                        .then_inc(xbo_ready, 1)
                if k in (8, 10):
                    split_lo((k - 8) // 2, slot_of((k - 8) // 2))
                if k == 13:
                    root_inverse(2, 1, 0)
            pool.wait_ge(comb_done, 1)
            link(pool.memset(plus_half[:, :], 0.5))
            pool.tensor_tensor(root[:, 0, :, :].rearrange("p t e -> p (t e)"),
                               comb[:, 0, :, :].rearrange("p t e -> p (t e)"),
                               plus_half[:, :], ALU.pow).then_inc(root_done, 1)
            root_inverse(3, 1, 1)

            def scale_x(n, slot, turn, h):
                m = 2 * (n - 1) + h
                pool.wait_ge(root_in[slot][h], 16 * turn)
                at_least(pool, xs_lo_done, m - 1)
                pool.tensor_tensor(xs[:, h, :], xn2_t[:, h, :], root_b[:, slot, h, :], ALU.mult)\
                    .then_inc(xs_done, 1)

            def network(n, slot, turn):
                if not isinstance(n, int) or n > 0:
                    scale_x(n, slot, turn, 1)
                    if not isinstance(n, int) or n < NN - 1:
                        split_lo(n + 1, 1 - slot)
                if not isinstance(n, int) or n < NN - 1:
                    scale_x(n + 1, 1 - slot, turn + (1 - (1 - slot)), 0)

            for n in range(NN):
                network(n, slot_of(n), (n + 1) // 2)

        @block.scalar
        def _(act):
            act.dma_start(small_sb[:, :],
                          bass.AP(tensor=small.tensor, offset=0, ap=[[0, H], [SMALL, HD], [1, SMALL]]))\
                .then_inc(small_in, 16)
            act.dma_start(ctx_sb[:, :], ctx_t).then_inc(ctx_in, 16)

            act.wait_ge(kv_done, 1)
            act.activation(k_t[:, :], ps[:, PROB_BANK[0], 0:B * SK], ACT.Copy).then_inc(kv_read, 1)
            act.activation(v_t[:, :, :].rearrange("p b k -> p (b k)"),
                           ps[:, PROB_BANK[0], 256:256 + B * SK], ACT.Copy).then_inc(kv_read, 1)

            def xn_high(b, bank):
                act.wait_ge(xt_done, b + 1)
                act.activation(xn_hi[:, b, :], ps[:, bank, :], ACT.Copy).then_inc(xn_hi_done, 1)

            xn_high(0, MISC_BANK)

            def exps(k):
                act.wait_ge(sub_done, k + 1)
                at_least(act, norm_done, k - 1)
                act.activation(prob[:, k % 2, :, :], s_sub[:, k % 2, :, :], ACT.Exp, scale=SCALE)\
                    .then_inc(exp_done, 1)

            def read_transposed(k):
                b, half, qt = k // UPB, k % UPB // TB, k % TB
                if b > 0:
                    act.wait_ge(pv_half, half + 1)
                at = 0
                for i, cnt in enumerate((3, CH - 3)):
                    act.wait_ge(pt_done, 2 * k + i + 1)
                    act.activation(prob_t[:, half, at:at + cnt, qt * P:(qt + 1) * P],
                                   ps[:, PROB_BANK[i], 0:cnt * P].rearrange("p (c q) -> p c q", q=P),
                                   ACT.Copy).then_inc(pt_read, 1)
                    at += cnt

            def read_attn(b):
                act.wait_ge(pv_half, 2 * b + 2)
                if b > 0:
                    act.wait_ge(proj_o, b)
                act.activation(attn_t[:, :], ps[:, PV_BANK, :], ACT.Copy).then_inc(attn_read, 1)

            def read_xn2(b):
                act.wait_ge(xt2_done, b + 1)
                act.activation(xn2_t[:, b, :], ps[:, MISC_BANK, :], ACT.Copy).then_inc(xn2_read, 1)

            def split_hi(n, slot):
                act.wait_ge(w_in[slot], 16)
                act.activation(w_hi[:, slot, :], w_raw[:, slot, :], ACT.Copy).then_inc(w_hi_done, 1)

            def router_exp(b):
                act.wait_ge(logit_read, b + 1)
                act.activation(r_exp[:, b, :, :], r_exp[:, b, :, :], ACT.Exp).then_inc(rexp_done, 1)

            for k in range(NU + 2):
                if k < NU:
                    exps(k)
                if k == 3:
                    xn_high(1, PV_BANK)
                if 3 <= k < 8:
                    r = k - 3
                    act.wait_ge(vt_done, r + 1)
                    act.activation(vblk[:, 4 * r:4 * r + 4, :],
                                   ps[:, MISC_BANK, :].rearrange("p (c q) -> p c q", q=P), ACT.Copy)\
                        .then_inc(vblk_ready, 1)
                if k >= 2:
                    read_transposed(k - 2)
                if k in (8, 9):
                    split_hi(k - 8, slot_of(k - 8))
                if k == 13:
                    read_attn(0)
            read_xn2(0)
            read_attn(1)
            router_exp(0)

            def relu(n, h, f):
                i = BPN * n + FT * h + f
                act.wait_ge(up_done, i + 1)
                at_least(act, square_done, i - 1)
                act.activation(hid_r[:, f % 2, :], ps[:, f, :], ACT.Relu).then_inc(relu_done, 1)

            def square(n, h, f):
                i = BPN * n + FT * h + f
                act.wait_ge(relu_done, i + 1)
                at_least(act, hid_lo_done, i - 1)
                act.activation(hid[:, f % 2, :], hid_r[:, f % 2, :], ACT.Square).then_inc(square_done, 1)

            def network(n):
                for h in range(B):
                    for f in range(FT):
                        relu(n, h, f)
                        square(n, h, f)
                        extra(n, h, f)

            def extra(n, h, f):
                if (n, h, f) == (0, 0, 2):
                    read_xn2(1)
                if (n, h, f) == (0, 1, 0):
                    router_exp(1)
                if (n, h, f) == (0, 1, 1):
                    act.wait_ge(root_t_done, 1)
                    act.activation(root_t[:, 0, :], ps[0:TB * NE, MISC_BANK, 0:P], ACT.Copy).then_inc(root_t_read, 1)
                if (n, h, f) == (1, 0, 1):
                    act.wait_ge(comb_done, 2)
                    act.activation(root[:, 1, :, :], comb[:, 1, :, :], ACT.Sqrt).then_inc(root_done, 1)
                if (n, h, f) == (1, 0, 2):
                    act.wait_ge(root_t_done, 2)
                    act.activation(root_t[:, 1, :], ps[0:TB * NE, MISC_BANK, 0:P], ACT.Copy).then_inc(root_t_read, 1)

            for n in range(NN):
                network(n)
            for h in range(B):
                act.wait_ge(down_done, NB if h else NB - FT)
                act.activation(y_t[:, h, :], ps[:, Y_BANK[h], :], ACT.Copy).then_inc(y_read, 1)

        @block.vector
        def _(dve):
            steps = [0]

            def link(ins):
                steps[0] += 1
                ins.then_inc(dve_step, 1)
                dve.wait_ge(dve_step, steps[0])

            def layer_norm_stats(which, src, g):
                for t in range(g * TB, (g + 1) * TB):
                    last = dve.bn_stats(stats[:, which, t, :], src[:, t, :])
                link(last)
                for t in range(g * TB, (g + 1) * TB):
                    last = dve.bn_aggr(mv[:, which, t, :], stats[:, which, t, :])
                link(last)
                dve.tensor_scalar(var_eps[:, which, g * TB:(g + 1) * TB], mv[:, which, g * TB:(g + 1) * TB, 1],
                                  EPS, None, ALU.add).then_inc(var_ready, 1)

            def layer_norm_apply(i, which, src, dst, g):
                dve.wait_ge(rstd_ready, i + 1)
                for t in range(g * TB, (g + 1) * TB):
                    last = dve.tensor_scalar(dst[:, t, :], src[:, t, :], mv[:, which, t, 0:1],
                                             rstd[:, which, t:t + 1], ALU.subtract, ALU.mult)
                last.then_inc(xn_ready, 1)

            def xn_low(b, bank):
                dve.wait_ge(xn_hi_done, b + 1)
                dve.tensor_tensor(xn_lo[:, b, :], ps[:, bank, :], xn_hi[:, b, :].bitcast(F32),
                                  ALU.subtract).then_inc(xn_lo_done, 1)

            dve.wait_ge(x_in[0], 16)
            layer_norm_stats(0, x_sb, 0)
            dve.wait_ge(bd_ready, 1)
            link(dve.tensor_reduce(group_mask[:, :], head_mask[:, :].rearrange("p (g j) -> p j g", j=JH),
                                   AX_X, ALU.add))
            layer_norm_apply(0, 0, x_sb, xn, 0)
            dve.wait_ge(kq_done, 1)
            link(dve.tensor_tensor(
                kblk[:, :, :, :],
                ps[:, PROB_BANK[1], 0:B * SK].rearrange("p (b k) -> p b k", k=SK).unsqueeze(2)
                .broadcast_to([P, B, JH, SK]),
                group_mask[:, :].unsqueeze(1).unsqueeze(3).broadcast_to([P, B, JH, SK]), ALU.mult))
            link(dve.tensor_copy(kblk_hi[:, :, :, :], kblk[:, :, :, :]))
            dve.tensor_tensor(kblk_lo[:, :, :, :], kblk[:, :, :, :], kblk_hi[:, :, :, :].bitcast(F32),
                              ALU.subtract).then_inc(kblk_ready, 1)
            xn_low(0, MISC_BANK)

            def scores_max(k):
                dve.wait_ge(score_done, k + 1)
                dve.tensor_reduce(s_max[:, k % 2, :].rearrange("p (g j) -> p g j", j=JH),
                                  ps[:, 2 * (k % 2):2 * (k % 2) + 2, 0:JH * SK]
                                  .rearrange("p g (j k) -> p g j k", k=SK), AX_X, ALU.max)\
                    .then_inc(max_done, 1)

            def scores_sub(k):
                dve.wait_ge(max_done, k + 1)
                at_least(dve, exp_done, k - 1)
                dve.tensor_tensor(s_sub[:, k % 2, :, :].rearrange("p (g j) k -> p g j k", j=JH),
                                  ps[:, 2 * (k % 2):2 * (k % 2) + 2, 0:JH * SK]
                                  .rearrange("p g (j k) -> p g j k", k=SK),
                                  s_max[:, k % 2, :].rearrange("p (g j) -> p g j", j=JH).unsqueeze(3)
                                  .broadcast_to([P, 2, JH, SK]), ALU.subtract).then_inc(sub_done, 1)

            def probs_sum(k):
                dve.wait_ge(exp_done, k + 1)
                dve.tensor_reduce(s_sum[:, k % 2, :], prob[:, k % 2, :, :], AX_X, ALU.add).then_inc(sum_done, 1)

            def probs_rec(k):
                dve.wait_ge(sum_done, k + 1)
                at_least(dve, norm_done, k - 1)
                dve.reciprocal(s_rec[:, k % 2, :], s_sum[:, k % 2, :]).then_inc(rec_done, 1)

            def residual(b):
                dve.wait_ge(proj_o, b + 1)
                dve.wait_ge(xbo_ready, 1)
                dve.tensor_tensor(x2[:, b * TB:(b + 1) * TB, :],
                                  ps[:, MISC_BANK, :].rearrange("p (t d) -> p t d", d=D),
                                  x_bo[:, b * TB:(b + 1) * TB, :], ALU.add).then_inc(x2_done, 1)
                dve.wait_ge(x2_done, b + 1)

            def split_x2(b):
                dve.wait_ge(xn2_read, b + 1)
                dve.tensor_copy(x2_hi[:, b, :], xn2_t[:, b, :]).then_inc(x2_hi_done, 1)
                dve.wait_ge(x2_hi_done, b + 1)
                dve.tensor_tensor(x2_lo[:, b, :], xn2_t[:, b, :], x2_hi[:, b, :].bitcast(F32), ALU.subtract)\
                    .then_inc(x2_lo_done, 1)

            for k in range(NU + 1):
                if k < NU:
                    scores_max(k)
                if k > 0:
                    probs_sum(k - 1)
                if k < NU:
                    scores_sub(k)
                if k > 0:
                    probs_rec(k - 1)
                if k == 0:
                    dve.wait_ge(x_in[1], 16)
                    layer_norm_stats(0, x_sb, 1)
                if k == 1:
                    layer_norm_apply(1, 0, x_sb, xn, 1)
                if k == 4:
                    xn_low(1, PV_BANK)
                if k == 13:
                    residual(0)
                    layer_norm_stats(1, x2, 0)
                if k == 14:
                    layer_norm_apply(2, 1, x2, xn2, 0)
            split_x2(0)

            def router_sub(b):
                dve.wait_ge(logit_done, b + 1)
                logits = ps[:, PV_BANK, 0:TB * NE].rearrange("p (t e) -> p t e", e=NE)
                link(dve.tensor_reduce(r_s[:, 0, :], logits, AX_X, ALU.max))
                dve.tensor_tensor(r_exp[:, b, :, :], logits,
                                  r_s[:, 0, :].unsqueeze(2).broadcast_to([P, TB, NE]), ALU.subtract)\
                    .then_inc(logit_read, 1)

            def over_experts(a):
                return a.unsqueeze(2).broadcast_to([P, TB, NE])

            def router_top2(b):
                dve.wait_ge(rexp_done, b + 1)
                order = prio[:, :].unsqueeze(1).broadcast_to([P, TB, NE])
                link(dve.tensor_reduce(r_s[:, 0, :], r_exp[:, b, :, :], AX_X, ALU.add))
                link(dve.reciprocal(r_s[:, 1, :], r_s[:, 0, :]))
                link(dve.tensor_tensor(r_p[:, :, :], r_exp[:, b, :, :], over_experts(r_s[:, 1, :]), ALU.mult))
                link(dve.tensor_reduce(r_s[:, 2, :], r_p[:, :, :], AX_X, ALU.max))
                link(dve.tensor_tensor(r_a[:, :, :], r_p[:, :, :], over_experts(r_s[:, 2, :]), ALU.is_equal))
                link(dve.tensor_tensor(r_a[:, :, :], r_a[:, :, :], order, ALU.mult))
                link(dve.tensor_reduce(r_s[:, 3, :], r_a[:, :, :], AX_X, ALU.max))
                link(dve.tensor_tensor(r_b[:, :, :], r_a[:, :, :], over_experts(r_s[:, 3, :]), ALU.is_equal))
                link(dve.scalar_tensor_tensor(r_a[:, :, :], r_b[:, :, :], -2.0, r_p[:, :, :], ALU.mult, ALU.add))
                link(dve.tensor_reduce(r_s[:, 4, :], r_a[:, :, :], AX_X, ALU.max))
                link(dve.tensor_tensor(r_a[:, :, :], r_a[:, :, :], over_experts(r_s[:, 4, :]), ALU.is_equal))
                link(dve.tensor_tensor(r_a[:, :, :], r_a[:, :, :], order, ALU.mult))
                link(dve.tensor_reduce(r_s[:, 5, :], r_a[:, :, :], AX_X, ALU.max))
                link(dve.tensor_tensor(r_a[:, :, :], r_a[:, :, :], over_experts(r_s[:, 5, :]), ALU.is_equal))
                link(dve.tensor_tensor(r_s[:, 6, :], r_s[:, 2, :], r_s[:, 4, :], ALU.add))
                link(dve.tensor_scalar(r_s[:, 6, :], r_s[:, 6, :], 1e-9, None, ALU.max))
                link(dve.reciprocal(r_s[:, 7, :], r_s[:, 6, :]))
                link(dve.tensor_tensor(r_a[:, :, :], r_a[:, :, :], r_b[:, :, :], ALU.add))
                link(dve.tensor_tensor(r_c[:, :, :], r_p[:, :, :], over_experts(r_s[:, 7, :]), ALU.mult))
                dve.tensor_tensor(comb[:, b, :, :], r_c[:, :, :], r_a[:, :, :], ALU.mult).then_inc(comb_done, 1)

            dve.wait_ge(const_ready, 1)
            router_sub(0)
            router_top2(0)

            def split_hid(n, h, f):
                i = BPN * n + FT * h + f
                dve.wait_ge(square_done, i + 1)
                at_least(dve, down_done, i - 3)
                dve.tensor_copy(hid_hi[:, f, :], hid[:, f % 2, :]).then_inc(hid_hi_done, 1)
                dve.wait_ge(hid_hi_done, i + 1)
                dve.tensor_tensor(hid_lo[:, f, :], hid[:, f % 2, :], hid_hi[:, f, :].bitcast(F32),
                                  ALU.subtract).then_inc(hid_lo_done, 1)

            def split_xs(n, h):
                m = 2 * (n - 1) + h
                dve.wait_ge(xs_done, m + 1)
                if not isinstance(n, int) or n > 1:
                    dve.wait_ge(up_done, FT * (2 * n + h - 1))
                dve.tensor_copy(xs_hi[:, h, :], xs[:, h, :]).then_inc(xs_hi_done, 1)
                dve.wait_ge(xs_hi_done, m + 1)
                dve.tensor_tensor(xs_lo[:, h, :], xs[:, h, :], xs_hi[:, h, :].bitcast(F32), ALU.subtract)\
                    .then_inc(xs_lo_done, 1)

            def split_w(n, slot, wturn):
                dve.wait_ge(w_in[slot], 16 * wturn)
                dve.wait_ge(down_done, BPN * (n - 1))
                dve.tensor_copy(w_hi[:, slot, :], w_raw[:, slot, :]).then_inc(w_hi_done, 1)

            def network(n, slot, wturn):
                for h in range(B):
                    for f in range(FT):
                        split_hid(n, h, f)
                        if (n, h, f) == (0, 0, 0):
                            residual(1)
                            layer_norm_stats(1, x2, 1)
                        if (n, h, f) == (0, 0, 1):
                            layer_norm_apply(3, 1, x2, xn2, 1)
                        if (n, h, f) == (0, 0, 2):
                            split_x2(1)
                        if (n, h, f) == (0, 0, 3):
                            router_sub(1)
                        if (n, h, f) == (0, 1, 0):
                            router_top2(1)
                        if h == 0 and f == 2 and n > 0:
                            split_xs(n, 1)
                        if h == 0 and f == 3 and 0 < n < NN - 1:
                            split_w(n + 1, 1 - slot, wturn)
                        if h == 1 and f == 2 and n < NN - 1:
                            split_xs(n + 1, 0)

            for n in range(NN):
                network(n, slot_of(n), (n + 1) // 2 + 1)
            for h in range(B):
                dve.wait_ge(y_t_done, h + 1)
                dve.tensor_tensor(y_out[:, h * TB:(h + 1) * TB, :],
                                  ps[:, (PV_BANK, MISC_BANK)[h], :].rearrange("p (t d) -> p t d", d=D),
                                  x2[:, h * TB:(h + 1) * TB, :], ALU.add).then_inc(y_ready, 1)

        @block.tensor
        def _(pe):
            def three(out_ap, w, wl, m, ml, start, stop):
                pe.matmul(out_ap, lhsT=w, rhs=m, start=start, stop=False)
                pe.matmul(out_ap, lhsT=w, rhs=ml, start=False, stop=False)
                return pe.matmul(out_ap, lhsT=wl, rhs=m, start=False, stop=stop)

            pe.wait_ge(bd_ready, 3)
            pe.wait_ge(ctx_in, 16)

            def bd_of(i):
                return bd[:, i, :, :].rearrange("p h e -> p (h e)")

            pe.matmul(ps[:, PROB_BANK[0], 0:B * SK], lhsT=bd_of(0), rhs=ctx_sb[:, :], start=True, stop=True)
            pe.matmul(ps[:, PROB_BANK[0], 256:256 + B * SK], lhsT=bd_of(2), rhs=ctx_sb[:, :],
                      start=True, stop=True).then_inc(kv_done, 1)
            pe.wait_ge(kv_read, 1)
            pe.matmul(ps[:, PROB_BANK[1], 0:B * SK], lhsT=bd_of(1), rhs=k_t[:, :],
                      start=True, stop=True).then_inc(kq_done, 1)

            def transpose_x(i, src, g, bank, done):
                pe.wait_ge(xn_ready, i + 1)
                for t in range(TB):
                    last = pe.transpose(ps[:, bank, t * P:(t + 1) * P], src[:, g * TB + t, :], ident[:, :])
                last.then_inc(done, 1)

            pe.wait_ge(ident_ready, 1)
            transpose_x(0, xn, 0, MISC_BANK, xt_done)
            pe.wait_ge(bias_ready, 1)

            def scores(k):
                b, half, qt = k // UPB, k % UPB // TB, k % TB
                if k % UPB == 0:
                    pe.wait_ge(xn_lo_done, b + 1)
                    pe.wait_ge(kblk_ready, 1)
                at_least(pe, sub_done, k - 1)
                for i in range(2):
                    g = 2 * half + i
                    r0, r1 = 32 * g, 32 * g + 32
                    dst = heads_of(2 * (k % 2) + i)
                    q = slice(qt * P, (qt + 1) * P)
                    pe.matmul(dst, lhsT=ident_bf[:, :],
                              rhs=mask_bias[:, b * TB + qt, :].unsqueeze(1).broadcast_to([P, JH, SK]),
                              start=True, stop=False)
                    last = three(dst, xn_hi[r0:r1, b, q], xn_lo[r0:r1, b, q],
                                 kblk_hi[r0:r1, b, :, :], kblk_lo[r0:r1, b, :, :], False, True)
                last.then_inc(score_done, 1)

            def transpose_probs(k):
                pe.wait_ge(norm_done, k + 1)
                pe.wait_ge(const_ready, 3)
                at_least(pe, pt_read, 2 * k)
                rows = prob_n[:, k % 2, :, :].rearrange("p h k -> p (h k)")
                for c in range(CH):
                    i, at = (0, c) if c < 3 else (1, c - 3)
                    ins = pe.transpose(ps[:, PROB_BANK[i], at * P:(at + 1) * P],
                                       rows[:, c * P:(c + 1) * P], ident[:, :])
                    if c in (2, CH - 1):
                        ins.then_inc(pt_done, 1)

            def pv(b, c):
                half = c // CH
                if c % CH == 0:
                    pe.wait_ge(pt_read, 2 * (UPB * b + TB * (half + 1)))
                    pe.wait_ge(vblk_ready, 5)
                    if b > 0 and c == 0:
                        pe.wait_ge(attn_read, b)
                ins = pe.matmul(ps[:, PV_BANK, :], lhsT=vblk[:, b * 2 * CH + c, :],
                                rhs=prob_t[:, half, c % CH, :], start=(c == 0), stop=(c == 2 * CH - 1))
                if c % CH == CH - 1:
                    ins.then_inc(pv_half, 1)

            def project_out(b):
                pe.wait_ge(attn_read, b + 1)
                if b == 0:
                    pe.wait_ge(wo_in, 16)
                    pe.wait_ge(vblk_ready, 5)
                else:
                    pe.wait_ge(xn2_read, b)
                for t in range(TB):
                    last = pe.matmul(ps[:, MISC_BANK, t * P:(t + 1) * P], lhsT=attn_t[:, t * P:(t + 1) * P],
                                     rhs=wo_sb[:, 0:D], start=True, stop=True)
                last.then_inc(proj_o, 1)

            pv_at = {7: (0, (0, 1)), 8: (0, (2, 3)), 9: (0, (4,)), 11: (0, (5, 6)), 12: (0, (7, 8)), 13: (0, (9,)),
                     15: (1, (0, 1)), 16: (1, (2, 3)), 17: (1, (4,))}
            for k in range(NU + 2):
                if k < NU:
                    scores(k)
                if k == 3:
                    transpose_x(1, xn, 1, PV_BANK, xt_done)
                if 3 <= k < 8:
                    r = k - 3
                    if r == 0:
                        pe.wait_ge(xn_lo_done, 1)
                        pe.wait_ge(vblk_t_ready, 1)
                    if r == 2:
                        pe.wait_ge(vblk_t_ready, 2)
                    at_least(pe, vblk_ready, r)
                    pe.wait_ge(const_ready, 2)
                    flat = vblk_t[:, :, :, :].rearrange("p b h k -> p (b h k)")
                    for j in range(4):
                        c = 4 * r + j
                        last = pe.transpose(ps[:, MISC_BANK, j * P:(j + 1) * P], flat[:, c * P:(c + 1) * P],
                                            ident[:, :])
                    last.then_inc(vt_done, 1)
                if k >= 2:
                    transpose_probs(k - 2)
                if k in pv_at:
                    b, chunks = pv_at[k]
                    if k == 7:
                        pe.wait_ge(xn_lo_done, 2)
                    for c in chunks:
                        pv(b, c)
                if k == 14:
                    project_out(0)
            pe.wait_ge(x2_done, 1)
            transpose_x(2, xn2, 0, MISC_BANK, xt2_done)
            for c in range(CH, 2 * CH):
                pv(1, c)

            def logits(b):
                pe.wait_ge(xn2_read, b + 1)
                if b == 0:
                    pe.wait_ge(attn_read, 2)
                for t in range(TB):
                    last = pe.matmul(ps[:, PV_BANK, t * NE:(t + 1) * NE], lhsT=xn2_t[:, b, t * P:(t + 1) * P],
                                     rhs=wo_sb[:, D:D + NE], start=True, stop=True)
                last.then_inc(logit_done, 1)

            def transpose_root(b):
                pe.wait_ge(root_done, b + 1)
                if b == 0:
                    pe.wait_ge(xn2_read, 2)
                else:
                    pe.wait_ge(root_t_read, b)
                pe.transpose(ps[0:TB * NE, MISC_BANK, 0:P], root[:, b, :, :].rearrange("p t e -> p (t e)"),
                             ident[:, :]).then_inc(root_t_done, 1)

            def up(n, slot, h, f):
                i = BPN * n + FT * h + f
                first = isinstance(n, int) and n == 0
                at_least(pe, relu_done, i - 3)
                if h == 0 and f == 0:
                    pe.wait_ge(w_lo_done, n + 1)
                if f == 0:
                    if first:
                        pe.wait_ge(x2_lo_done, h + 1)
                    else:
                        pe.wait_ge(xs_lo_done, 2 * (n - 1) + h + 1)
                hi, lo = (x2_hi, x2_lo) if first else (xs_hi, xs_lo)
                w = slice(f * P, (f + 1) * P)
                three(ps[:, f, :], w_hi[:, slot, w], w_lo[:, slot, w], hi[:, h, :], lo[:, h, :], True, True)\
                    .then_inc(up_done, 1)

            def down(n, slot, h, f):
                i = BPN * n + FT * h + f
                pe.wait_ge(hid_lo_done, i + 1)
                w = slice(FF + f * P, FF + (f + 1) * P)
                three(ps[:, Y_BANK[h], :], w_hi[:, slot, w], w_lo[:, slot, w], hid_hi[:, f, :], hid_lo[:, f, :],
                      isinstance(n, int) and n == 0 and f == 0, isinstance(n, int) and n == NN - 1 and f == FT - 1)\
                    .then_inc(down_done, 1)

            def network(n, slot):
                for j in range(BPN):
                    up(n, slot, j // FT, j % FT)
                    if j >= LAG:
                        down(n, slot, (j - LAG) // FT, (j - LAG) % FT)
                    elif not isinstance(n, int) or n > 0:
                        down(n - 1, 1 - slot, 1, j + FT - LAG)
                    extra(n, j)

            def extra(n, j):
                if (n, j) == (0, 0):
                    project_out(1)
                if (n, j) == (0, 2):
                    pe.wait_ge(x2_done, 2)
                    transpose_x(3, xn2, 1, MISC_BANK, xt2_done)
                if (n, j) == (0, 3):
                    logits(1)
                if (n, j) == (0, 5):
                    transpose_root(0)
                if (n, j) == (1, 1):
                    transpose_root(1)

            logits(0)
            pe.wait_ge(sub_done, NU)
            pe.wait_ge(pt_read, 2 * NU)
            for n in range(NN):
                network(n, slot_of(n))
            for f in range(FT - LAG, FT):
                down(NN - 1, slot_of(NN - 1), 1, f)
            for h in range(B):
                pe.wait_ge(y_read, h + 1)
                bank = (PV_BANK, MISC_BANK)[h]
                for t in range(TB):
                    last = pe.transpose(ps[:, bank, t * P:(t + 1) * P], y_t[:, h, t * P:(t + 1) * P], ident[:, :])
                last.then_inc(y_t_done, 1)


def kernel(x, ctx_1024, mask_Bx1xSxS2_ik1, L0_xattn_Wv, L0_xattn_Wk, L0_xattn_Wq, L0_xattn_Wo, L0_xattn_bo,
           L0_ffn_router_w, L0_ffn_w_fc, L0_ffn_w_proj, L0_ffn_shared_fc, L0_ffn_shared_proj):
    import numpy as np
    import concourse.bacc as bacc
    from concourse.bass_utils import run_bass_kernel_spmd

    up = np.concatenate([np.asarray(L0_ffn_shared_fc)[None], np.asarray(L0_ffn_w_fc)]).transpose(0, 2, 1)
    down = np.concatenate([np.asarray(L0_ffn_shared_proj)[None], np.asarray(L0_ffn_w_proj)])
    down = down.reshape(NN, D, FT, P).transpose(0, 3, 2, 1).reshape(NN, P, FF)
    arrays = {
        "x": np.asarray(x).reshape(B * S, D),
        "ctx_t": np.asarray(ctx_1024).transpose(2, 0, 1).reshape(D, B * SK),
        "mask": np.asarray(mask_Bx1xSxS2_ik1).reshape(B * S, SK),
        "small": np.concatenate([np.asarray(L0_xattn_Wk).T, np.asarray(L0_xattn_Wq), np.asarray(L0_xattn_Wv).T],
                                axis=1),
        "wo_r": np.concatenate([np.asarray(L0_xattn_Wo).T, np.asarray(L0_ffn_router_w).T], axis=1),
        "bo": np.asarray(L0_xattn_bo),
        "w_all": np.concatenate([up, down], axis=2),
    }
    nc = bacc.Bacc("TRN2", target_bir_lowering=False, num_devices=1)
    args = []
    for name, a in arrays.items():
        arrays[name] = a = np.ascontiguousarray(a)
        args.append(nc.dram_tensor(name, a.shape, mybir.dt.from_np(a.dtype), kind="ExternalInput").ap())
    args.append(nc.dram_tensor("out", (B * S, D), F32, kind="ExternalOutput").ap())
    xattn_moe(nc, *args)
    r = run_bass_kernel_spmd(nc, [arrays], core_ids=[0])
    return r.results[0]["out"].reshape(B, S, D)
```

```python
from collections import namedtuple
from contextlib import ExitStack

import concourse.bass as bass
from concourse import mybir

F32 = mybir.dt.float32
F32R = mybir.dt.float32r
BF16 = mybir.dt.bfloat16
I32 = mybir.dt.int32
ALU = mybir.AluOpType
ACT = mybir.ActivationFunctionType
AX_X = mybir.AxisListType.X

P = 128
B, S, D = 2, 512, 128
NT = B * S // P
TB = S // P
H, HD = 16, 8
SK = 77
SKP = 80
UH = H // 2
JH = 4
NU = NT * 2
UPB = TB * 2
CH = UH * SKP // P
NE = 8
NN = NE + 1
FF = 512
FT = FF // P
BPN = B * FT
NB = NN * BPN
LAG = 6
LOOP = (4, 2)
TLAG = 3
PNR = 4
WARM = 9
EPS = 1e-5
MASKED = -1e20
SCALE = 1.0 / float(D) ** 0.5
SMALL = 3 * HD


Net = namedtuple("Net", "n half odd")


def net(n):
    return Net(n, n // 2, n % 2)


def following(m):
    return Net(m.n + 1, m.half + 1 if m.odd else m.half, 1 - m.odd)


def preceding(m):
    return Net(m.n - 1, m.half if m.odd else m.half - 1, 1 - m.odd)


def slot_of(m):
    return 1 - m.odd


def known(m):
    return isinstance(m.n, int)


UNITS = [(n, h) for h in range(B) for n in range(3)] + \
    [(n, h) for n in range(3, NN) for h in range(B)]
BLOCKS = [(net(n), h, f) for n, h in UNITS for f in range(FT)]
EARLY = 3 * BPN


def number(block):
    m, h, f = block
    if known(m):
        return UNITS.index((m.n, h)) * FT + f
    return BPN * m.n + FT * h + f


def back(block, d):
    m, h, f = block
    if known(m):
        return BLOCKS[number(block) - d]
    q = FT * h + f - d
    return (m, q // FT, q % FT) if q >= 0 else (preceding(m), (q + BPN) // FT, (q + BPN) % FT)


def place(block):
    m, h, f = block
    return number(block) % BPN if known(m) else FT * h + f


def on_pool(block):
    m, h, f = block
    return f == FT - 1 or (known(m) and BPN * m.n < EARLY and f == 1)


def low_count(block):
    m, h, f = block
    if known(m):
        return sum(on_pool(b) == on_pool(block) for b in BLOCKS[:number(block) + 1])
    early = EARLY // FT
    if on_pool(block):
        return early + 2 * m.n + h + 1
    return 3 * (2 * m.n + h) + f + 1 - early


def xs_number(m, h):
    return 2 * h + m.n - 1 if known(m) and m.n < 3 else 2 * (m.n - 1) + h


def xattn_moe(nc, x, ctx_t, mask, small, wo_r, bo, w_all, out):
    ctx = ExitStack()
    with ctx:
        def sb(name, shape, dt):
            return ctx.enter_context(nc.sbuf_tensor(name, shape, dt))

        def sem(name):
            return ctx.enter_context(nc.semaphore(name))

        root_dram = nc.dram_tensor("root_dram", (NE, B * S), F32).ap()

        x_sb = sb("x_sb", [P, NT, D], F32)
        ctx_sb = sb("ctx_sb", [P, B * SK], F32)
        mask_sb = sb("mask_sb", [P, NT, SK], I32)
        small_sb = sb("small_sb", [P, SMALL], F32)
        wo_sb = sb("wo_sb", [P, D + NE], F32)
        bo_sb = sb("bo_sb", [P, D], F32)
        ident = sb("ident", [P, P], F32)
        ident_bf = sb("ident_bf", [P, P], BF16)
        head_mask = sb("head_mask", [P, H], F32)
        warm = sb("warm", [P, 512], BF16)
        minus_half = sb("minus_half", [P, TB], F32)
        prio = sb("prio", [P, NE], F32)
        stats = sb("stats", [P, 2, NT, 6], F32)
        mv = sb("mv", [P, 2, NT, 2], F32)
        var_eps = sb("var_eps", [P, 2, NT], F32)
        rstd = sb("rstd", [P, 2, NT], F32)
        xn = sb("xn", [P, NT, D], F32)
        xn_hi = sb("xn_hi", [P, B, S], F32R)
        xn_lo = sb("xn_lo", [P, B, S], F32R)
        shared = sb("shared", [P, 2 * BPN * S], F32R)
        kb = B * H * SK
        kblk_hi = shared[:, 0:kb].rearrange("p (b h k) -> p b h k", b=B, h=H)
        kblk_lo = shared[:, kb:2 * kb].rearrange("p (b h k) -> p b h k", b=B, h=H)
        hid_hi = shared[:, 0:BPN * S].rearrange("p (i s) -> p i s", i=BPN)
        hid_lo = shared[:, BPN * S:2 * BPN * S].rearrange("p (i s) -> p i s", i=BPN)
        bd = sb("bd", [P, 3, H, HD], F32)
        k_t = sb("k_t", [P, B * SK], F32)
        v_t = sb("v_t", [P, B, SK], F32)
        vblk_t = sb("vblk_t", [P, B, H, SKP], F32)
        kq_hi = sb("kq_hi", [P, B, SK], F32R)
        kq_lo = sb("kq_lo", [P, B, SK], F32R)
        vblk = sb("vblk", [P, B * 2 * CH, P], F32)
        mask_bias = sb("mask_bias", [P, NT, SK], BF16)
        s_max = sb("s_max", [P, 2, UH], F32)
        s_sum = sb("s_sum", [P, 2, UH], F32)
        s_rec = sb("s_rec", [P, 2, UH], F32)
        s_sub = sb("s_sub", [P, 2, UH, SK], F32)
        prob = sb("prob", [P, 2, UH, SK], F32)
        prob_n = sb("prob_n", [P, PNR, UH, SKP], F32)
        prob_t = sb("prob_t", [P, 2, CH, S], F32)
        attn_t = sb("attn_t", [P, S], F32)
        x_bo = sb("x_bo", [P, NT, D], F32)
        x2 = sb("x2", [P, NT, D], F32)
        xn2 = sb("xn2", [P, NT, D], F32)
        xn2_t = sb("xn2_t", [P, B, S], F32)
        x2_hi = sb("x2_hi", [P, B, S], F32R)
        x2_lo = sb("x2_lo", [P, B, S], F32R)
        r_exp = sb("r_exp", [P, B, TB, NE], F32)
        r_p = sb("r_p", [P, TB, NE], F32)
        r_a = sb("r_a", [P, TB, NE], F32)
        r_s = sb("r_s", [P, 8, TB], F32)
        r_sel = sb("r_sel", [P, B, 2, TB, NE], F32)
        r_w = sb("r_w", [P, B, 2, TB], F32)
        r_term = sb("r_term", [P, 2, TB, NE], F32)
        half = sb("half", [P, 2, TB], F32)
        root = sb("root", [P, B, TB, NE], F32)
        root_t = sb("root_t", [TB * NE, B, P], F32)
        w_raw = sb("w_raw", [P, 2, 2 * FF], F32)
        w_hi = sb("w_hi", [P, 2, 2 * FF], F32R)
        w_lo = sb("w_lo", [P, 2, 2 * FF], F32R)
        w_hi_2 = xn_hi[:, :, :].rearrange("p b s -> p (b s)")
        w_lo_2 = xn_lo[:, :, :].rearrange("p b s -> p (b s)")
        root_b = sb("root_b", [P, 2, B, S], F32)
        xs = sb("xs", [P, B, S], F32)
        xs_hi = sb("xs_hi", [P, B, S], F32R)
        xs_lo = sb("xs_lo", [P, B, S], F32R)
        hid_r = sb("hid_r", [P, 2, S], F32)
        hid = sb("hid", [P, FT, S], F32)
        y_t = prob_t[:, 0, 0:B, :]
        y_out = xn

        ps = ctx.enter_context(nc.psum_tensor("ps", [P, 8, 512], F32))
        PROB_BANK = (4, 5)
        Y_BANK = (4, 5)
        PV_BANK, MISC_BANK = 6, 7
        ROOT_BANK = (6, 7)
        SPREAD_BANK = (5, 6)
        X_BANK = (6, 7, 4, 5)

        x_in = [sem("x_in0"), sem("x_in1")]
        mask_in = [sem("mask_in0"), sem("mask_in1")]
        ctx_in, small_in, wo_in, bo_in = (sem(n) for n in ("ctx_in", "small_in", "wo_in", "bo_in"))
        w_in = [[sem(f"w_in{q}{part}") for part in ("up", "down")] for q in range(2)]
        root_in = [[sem(f"root_in{q}{h}") for h in range(B)] for q in range(2)]
        root_out = [sem("root_out0"), sem("root_out1")]
        out_done = sem("out_done")
        pool_step, dve_step = sem("pool_step"), sem("dve_step")
        ident_ready, const_ready, bd_ready, head_ready = (sem(n) for n in (
            "ident_ready", "const_ready", "bd_ready", "head_ready"))
        bias_ready, xbo_ready, vblk_t_ready = sem("bias_ready"), sem("xbo_ready"), sem("vblk_t_ready")
        var_ready, rstd_ready, xn_ready = sem("var_ready"), sem("rstd_ready"), sem("xn_ready")
        xt_done, xn_hi_done, xn_lo_done = sem("xt_done"), sem("xn_hi_done"), sem("xn_lo_done")
        kv_done, kv_read, kq_done, kq_split, warm_ready = (sem(n) for n in (
            "kv_done", "kv_read", "kq_done", "kq_split", "warm_ready"))
        kblk_ready = [[sem(f"kblk_ready{b}{half}") for half in range(2)] for b in range(B)]
        vt_done, vblk_ready = sem("vt_done"), sem("vblk_ready")
        score_done, max_done, sub_done, exp_done, sum_done, rec_done, norm_done = (sem(n) for n in (
            "score_done", "max_done", "sub_done", "exp_done", "sum_done", "rec_done", "norm_done"))
        pt_done, pt_read, pv_half, attn_read, proj_o = (sem(n) for n in (
            "pt_done", "pt_read", "pv_half", "attn_read", "proj_o"))
        x2_done, xt2_done, xn2_read, x2_hi_done, x2_lo_done = (sem(n) for n in (
            "x2_done", "xt2_done", "xn2_read", "x2_hi_done", "x2_lo_done"))
        logit_done, logit_read, rexp_done, top2_done, root_done, root_t_done, root_t_read = (
            sem(n) for n in ("logit_done", "logit_read", "rexp_done", "top2_done", "root_done",
                             "root_t_done", "root_t_read"))
        spread_done = sem("spread_done")
        w_hi_done = [sem("w_hi_done_up"), sem("w_hi_done_down")]
        w_lo_done = [sem("w_lo_done_up"), sem("w_lo_done_down")]
        xs_first_done = sem("xs_first_done")
        xs_done, xs_hi_done, xs_lo_done = sem("xs_done"), sem("xs_hi_done"), sem("xs_lo_done")
        hid_lo_pool_done = sem("hid_lo_pool_done")
        up_done, relu_done, square_done, hid_hi_done, hid_lo_done, down_done = (sem(n) for n in (
            "up_done", "relu_done", "square_done", "hid_hi_done", "hid_lo_done", "down_done"))
        y_read, y_t_done, y_ready = sem("y_read"), sem("y_t_done"), sem("y_ready")

        def at_least(eng, s, n):
            if not isinstance(n, int) or n > 0:
                eng.wait_ge(s, n)

        def heads_of(bank):
            return ps[:, bank, 0:JH * SK].rearrange("p (j k) -> p j k", k=SK)

        def wait_low(eng, b):
            eng.wait_ge(hid_lo_pool_done if on_pool(b) else hid_lo_done, low_count(b))

        def part_of(part):
            return slice(part * FF, (part + 1) * FF)

        UP, DOWN = 0, 1

        def split_weights(m):
            if known(m) and m.n == 2:
                return w_hi_2, w_lo_2
            return w_hi[:, slot_of(m), :], w_lo[:, slot_of(m), :]

        def split_input(m, h):
            if known(m) and m.n in (0, 2):
                at = h if m.n == 0 else 0
                return x2_hi[:, at, :], x2_lo[:, at, :]
            return xs_hi[:, h, :], xs_lo[:, h, :]

        def run_networks(eng, network):
            first, pairs = LOOP
            for n in range(3, first):
                network(net(n))
            with eng.Fori(0, pairs) as k:
                network(Net(2 * k + first, k + first // 2, 0))
                network(Net(2 * k + first + 1, k + first // 2, 1))
            for n in range(first + 2 * pairs, NN):
                network(net(n))

        def key_blocks(eng, dst, src, b, half):
            heads = slice(half * UH, half * UH + UH)
            eng.wait_ge(kq_split, 2)
            eng.tensor_tensor(dst[:, b, heads, :],
                              src[:, b, :].bitcast(F32).unsqueeze(1).broadcast_to([P, UH, SK]),
                              head_mask[:, heads].unsqueeze(2).broadcast_to([P, UH, SK]), ALU.mult)\
               .then_inc(kblk_ready[b][half], 1)

        block = ctx.enter_context(nc.Block())

        @block.sync
        def _(sp):
            x_v = x.rearrange("(t p) d -> p t d", p=P)
            sp.dma_start(x_sb[:, 0:TB, :], x_v[:, 0:TB, :]).then_inc(x_in[0], 16)
            sp.dma_start(ctx_sb[:, :], ctx_t).then_inc(ctx_in, 16)
            mask_v = mask.rearrange("(t p) k -> p t k", p=P)
            for b in range(B):
                sp.dma_start(mask_sb[:, b * TB:(b + 1) * TB, :], mask_v[:, b * TB:(b + 1) * TB, :])\
                  .then_inc(mask_in[b], 16)
            sp.dma_start(x_sb[:, TB:NT, :], x_v[:, TB:NT, :]).then_inc(x_in[1], 16)
            sp.dma_start(wo_sb[:, :], wo_r).then_inc(wo_in, 16)
            sp.dma_start(bo_sb[:, :], bo.partition_broadcast(P)).then_inc(bo_in, 16)

            def load_w(m, part):
                slot = slot_of(m)
                at_least(sp, w_lo_done[part], m.n - 1)
                sp.dma_start(w_raw[:, slot, part_of(part)], w_all[m.n, :, part_of(part)])\
                  .then_inc(w_in[slot][part], 16)

            def load_root(m, h):
                slot = slot_of(m)
                at_least(sp, xs_done, 2 * (m.n - 4) + h + 1)
                sp.dma_start(root_b[:, slot, h, :],
                             root_dram[m.n - 1, h * S:(h + 1) * S].partition_broadcast(P))\
                  .then_inc(root_in[slot][h], 16)

            for n in range(4):
                load_w(net(n), UP)
                load_w(net(n), DOWN)
            for h in range(B):
                sp.wait_ge(root_t_read, h + 1)
                sp.dma_start(root_dram.rearrange("e (b t p) -> b t e p", b=B, t=TB)[h, :, :, :],
                             root_t[:, h, :]).then_inc(root_out[h], 16)
                sp.wait_ge(root_out[h], 16)
                for n in (2, 3):
                    load_root(net(n), h)
            for n in range(4, NN):
                load_w(net(n), UP)
                for h in range(B):
                    load_root(net(n), h)
                load_w(net(n), DOWN)
            out_v = out.rearrange("(t p) d -> p t d", p=P)
            for h in range(B):
                sp.wait_ge(y_ready, h + 1)
                sp.dma_start(out_v[:, h * TB:(h + 1) * TB, :], y_out[:, h * TB:(h + 1) * TB, :])\
                  .then_inc(out_done, 16)
            sp.wait_ge(out_done, 16 * B)

        @block.gpsimd
        def _(pool):
            steps = [0]

            def link(ins):
                steps[0] += 1
                ins.then_inc(pool_step, 1)
                pool.wait_ge(pool_step, steps[0])

            link(pool.memset(head_mask[:, :], 1.0))
            link(pool.affine_select(out=head_mask[:, :], in_=head_mask[:, :], compare_op=ALU.is_ge, fill=0.0,
                                    base=0, pattern=[[-HD, H]], channel_multiplier=1))
            pool.affine_select(out=head_mask[:, :], in_=head_mask[:, :], compare_op=ALU.is_ge, fill=0.0,
                               base=HD - 1, pattern=[[HD, H]], channel_multiplier=-1).then_inc(head_ready, 1)
            link(pool.memset(ident[:, :], 0.0))
            pool.affine_select(out=ident[:, :], in_=ident[:, :], compare_op=ALU.not_equal, fill=1.0,
                               base=0, pattern=[[-1, P]], channel_multiplier=1).then_inc(ident_ready, 1)
            pool.memset(half[:, :, :], 0.5)
            link(pool.memset(minus_half[:, :], -0.5))

            def root_inverse(i, which, g):
                pool.wait_ge(var_ready, i + 1)
                pool.tensor_tensor(rstd[:, which, g * TB:(g + 1) * TB], var_eps[:, which, g * TB:(g + 1) * TB],
                                   minus_half[:, :], ALU.pow).then_inc(rstd_ready, 1)

            def mask_to_bias(b):
                pool.wait_ge(mask_in[b], 16)
                pool.tensor_scalar(mask_bias[:, b * TB:(b + 1) * TB, :], mask_sb[:, b * TB:(b + 1) * TB, :],
                                   0.0, MASKED, ALU.is_equal, ALU.mult).then_inc(bias_ready, 1)

            pool.wait_ge(ident_ready, 1)
            pool.tensor_copy(ident_bf[:, :], ident[:, :]).then_inc(ident_ready, 1)
            root_inverse(0, 0, 0)
            mask_to_bias(0)
            key_blocks(pool, kblk_lo, kq_lo, 0, 0)
            for i in range(NE):
                last = pool.memset(prio[:, i:i + 1], float(NE - i))
            last.then_inc(const_ready, 1)
            pool.memset(vblk_t[:, :, :, SK:SKP], 0.0).then_inc(const_ready, 1)
            pool.memset(prob_n[:, :, :, SK:SKP], 0.0).then_inc(const_ready, 1)
            root_inverse(1, 0, 1)

            def normalise(k):
                pool.wait_ge(rec_done, k + 1)
                at_least(pool, pt_done, 2 * (k - PNR + 1))
                pool.tensor_tensor(prob_n[:, k % PNR, :, 0:SK], prob[:, k % 2, :, :],
                                   s_rec[:, k % 2, :].unsqueeze(2).broadcast_to([P, UH, SK]),
                                   ALU.mult).then_inc(norm_done, 1)

            def v_blocks(b):
                pool.wait_ge(kv_read, 2)
                pool.tensor_tensor(vblk_t[:, b, :, 0:SK], v_t[:, b, :].unsqueeze(1).broadcast_to([P, H, SK]),
                                   head_mask[:, :].unsqueeze(2).broadcast_to([P, H, SK]),
                                   ALU.mult).then_inc(vblk_t_ready, 1)

            def split_lo(m, part):
                at = part_of(part)
                hi, lo = split_weights(m)
                pool.wait_ge(w_hi_done[part], m.n + 1)
                pool.tensor_tensor(lo[:, at], w_raw[:, slot_of(m), at], hi[:, at].bitcast(F32),
                                   ALU.subtract).then_inc(w_lo_done[part], 1)

            for k in range(NU):
                normalise(k)
                if k == 4:
                    mask_to_bias(1)
                if k in (5, 8):
                    key_blocks(pool, kblk_lo, kq_lo, 1, k // 8)
                if k in (0, 2):
                    v_blocks(k // 2)
                if k == 12:
                    pool.wait_ge(bo_in, 16)
                    pool.wait_ge(x_in[0], 16)
                    pool.wait_ge(x_in[1], 16)
                    pool.tensor_tensor(x_bo[:, :, :], x_sb[:, :, :],
                                       bo_sb[:, :].unsqueeze(1).broadcast_to([P, NT, D]), ALU.add)\
                        .then_inc(xbo_ready, 1)
                if k in (8, 9, 10, 11):
                    split_lo(net((k - 8) // 2), k % 2)
                if k == 15:
                    root_inverse(2, 1, 0)

            def roots(b):
                pool.wait_ge(top2_done, b + 1)
                link(pool.tensor_tensor(r_w[:, b, :, :], r_w[:, b, :, :], half[:, :, :], ALU.pow))
                link(pool.tensor_tensor(r_term[:, :, :, :], r_sel[:, b, :, :, :],
                                        r_w[:, b, :, :].unsqueeze(3).broadcast_to([P, 2, TB, NE]), ALU.mult))
                pool.tensor_tensor(root[:, b, :, :], r_term[:, 0, :, :], r_term[:, 1, :, :], ALU.add)\
                    .then_inc(root_done, 1)
                pool.wait_ge(root_done, b + 1)

            def scale_x(m, h):
                pool.wait_ge(root_in[slot_of(m)][h], 16 * m.half)
                pool.wait_ge(xs_lo_done, xs_number(preceding(m), h) + 1)
                pool.tensor_tensor(xs[:, h, :], xn2_t[:, h, :], root_b[:, slot_of(m), h, :], ALU.mult)\
                    .then_inc(xs_done, 1)

            def hid_low(b):
                pool.wait_ge(hid_hi_done, number(b) + 1)
                pool.tensor_tensor(hid_lo[:, place(b), :], hid[:, b[2], :], hid_hi[:, place(b), :].bitcast(F32),
                                   ALU.subtract).then_inc(hid_lo_pool_done, 1)

            def x2_low(b):
                pool.wait_ge(x2_hi_done, b + 1)
                pool.tensor_tensor(x2_lo[:, b, :], xn2_t[:, b, :], x2_hi[:, b, :].bitcast(F32), ALU.subtract)\
                    .then_inc(x2_lo_done, 1)

            x2_low(0)
            split_lo(net(2), UP)
            split_lo(net(2), DOWN)
            roots(0)
            for i in range(1, EARLY - 1, 2):
                hid_low(BLOCKS[i])
                if i == 3:
                    root_inverse(3, 1, 1)
                    scale_x(net(2), 0)
                if i == 7:
                    roots(1)
                if i == 11:
                    scale_x(net(2), 1)
                if i == 15:
                    scale_x(net(3), 0)
                if i == 19:
                    split_lo(net(3), UP)
            scale_x(net(3), 1)

            def network(m):
                last = known(m) and m.n == NN - 1
                early = known(m) and m.n == 3
                if not last:
                    scale_x(following(m), 0)
                if not early:
                    split_lo(m, DOWN)
                hid_low(back((m, 0, 0), 1))
                if early:
                    split_lo(m, DOWN)
                if not last:
                    split_lo(following(m), UP)
                    scale_x(following(m), 1)
                hid_low((m, 0, FT - 1))

            run_networks(pool, network)
            hid_low(BLOCKS[NB - 1])

        @block.scalar
        def _(act):
            act.dma_start(small_sb[:, :],
                          bass.AP(tensor=small.tensor, offset=0, ap=[[0, H], [SMALL, HD], [1, SMALL]]))\
                .then_inc(small_in, 16)

            act.wait_ge(kv_done, 1)
            act.activation(k_t[:, :], ps[:, PROB_BANK[0], 0:B * SK], ACT.Copy).then_inc(kv_read, 1)
            act.activation(v_t[:, :, :].rearrange("p b k -> p (b k)"),
                           ps[:, PROB_BANK[0], 256:256 + B * SK], ACT.Copy).then_inc(kv_read, 1)

            for t in range(TB):
                act.wait_ge(xt_done, t + 1)
                act.activation(xn_hi[:, 0, t * P:(t + 1) * P], ps[:, X_BANK[t], 0:P], ACT.Copy)\
                    .then_inc(xn_hi_done, 1)

            def spread_keys(dst, src, b, half):
                act.wait_ge(kq_split, 2)
                for head in range(half * UH, half * UH + UH):
                    last = act.activation(dst[:, b, head, :], src[:, b, :].bitcast(F32), ACT.Copy,
                                          scale=head_mask[:, head:head + 1])
                last.then_inc(kblk_ready[b][half], 1)

            spread_keys(kblk_hi, kq_hi, 0, 1)
            spread_keys(kblk_lo, kq_lo, 0, 1)

            def exps(k):
                act.wait_ge(sub_done, k + 1)
                at_least(act, norm_done, k - 1)
                act.activation(prob[:, k % 2, :, :], s_sub[:, k % 2, :, :], ACT.Exp, scale=SCALE)\
                    .then_inc(exp_done, 1)

            def read_transposed(k):
                b, half, qt = k // UPB, k % UPB // TB, k % TB
                if b > 0:
                    act.wait_ge(pv_half, half + 1)
                at = 0
                for i, cnt in enumerate((3, CH - 3)):
                    act.wait_ge(pt_done, 2 * k + i + 1)
                    act.activation(prob_t[:, half, at:at + cnt, qt * P:(qt + 1) * P],
                                   ps[:, PROB_BANK[i], 0:cnt * P].rearrange("p (c q) -> p c q", q=P),
                                   ACT.Copy).then_inc(pt_read, 1)
                    at += cnt

            def read_attn(b):
                act.wait_ge(pv_half, 2 * b + 2)
                if b > 0:
                    act.wait_ge(proj_o, b)
                act.activation(attn_t[:, :], ps[:, PV_BANK, :], ACT.Copy).then_inc(attn_read, 1)

            def read_xn2(b):
                act.wait_ge(xt2_done, TB * (b + 1))
                act.activation(xn2_t[:, b, :], ps[:, MISC_BANK, :], ACT.Copy).then_inc(xn2_read, 1)
                if b == 0:
                    act.wait_ge(xn2_read, b + 1)
                    act.activation(x2_hi[:, b, :], xn2_t[:, b, :], ACT.Copy).then_inc(x2_hi_done, 1)

            def split_hi(m, part):
                slot, at = slot_of(m), part_of(part)
                act.wait_ge(w_in[slot][part], 16 * (m.half + 1))
                if known(m) and m.n == 2:
                    act.wait_ge(score_done, NU)
                elif not known(m) or m.n > 2:
                    before = preceding(preceding(m))
                    act.wait_ge((up_done, down_done)[part], number((before, B - 1, FT - 1)) + 1)
                act.activation(split_weights(m)[0][:, at], w_raw[:, slot, at], ACT.Copy)\
                    .then_inc(w_hi_done[part], 1)

            def router_exp(b):
                act.wait_ge(logit_read, b + 1)
                act.activation(r_exp[:, b, :, :], r_exp[:, b, :, :], ACT.Exp).then_inc(rexp_done, 1)

            for k in range(NU + TLAG):
                if k >= TLAG:
                    read_transposed(k - TLAG)
                if k == 16:
                    read_attn(0)
                if k < NU:
                    exps(k)
                if k in (1, 2):
                    spread_keys(kblk_hi, kq_hi, 1, k - 1)
                if k == 6:
                    act.wait_ge(xt_done, NT)
                    act.activation(xn_hi[:, 1, :], ps[:, PV_BANK, :], ACT.Copy).then_inc(xn_hi_done, 1)
                if 3 <= k < 8:
                    r = k - 3
                    act.wait_ge(vt_done, r + 1)
                    act.activation(vblk[:, 4 * r:4 * r + 4, :],
                                   ps[:, MISC_BANK, :].rearrange("p (c q) -> p c q", q=P), ACT.Copy)\
                        .then_inc(vblk_ready, 1)
                if k in (8, 9, 10, 11):
                    split_hi(net((k - 8) // 2), k % 2)
                if k in (16, 17):
                    split_hi(net(2), k % 2)
            read_xn2(0)

            def relu(b):
                i, f = number(b), b[2]
                act.wait_ge(up_done, i + 1)
                at_least(act, square_done, i - 1)
                act.activation(hid_r[:, f % 2, :], ps[:, f, :], ACT.Relu).then_inc(relu_done, 1)

            def square(b):
                i, f = number(b), b[2]
                act.wait_ge(relu_done, i + 1)
                if not isinstance(i, int) or i >= FT:
                    wait_low(act, back(b, FT))
                act.activation(hid[:, f, :], hid_r[:, f % 2, :], ACT.Square).then_inc(square_done, 1)

            def read_root(b):
                act.wait_ge(root_t_done, b + 1)
                act.activation(root_t[:, b, :], ps[0:TB * NE, ROOT_BANK[b], 0:P], ACT.Copy).then_inc(root_t_read, 1)

            router_exp(0)
            read_attn(1)
            for i in range(EARLY):
                relu(BLOCKS[i])
                if i not in (0, FT):
                    square(BLOCKS[i - 1])
                if i == FT - 1:
                    square(BLOCKS[i])
                    read_root(0)
                if i == 7:
                    read_xn2(1)
                    router_exp(1)
                if i == 13:
                    read_root(1)
                if i == 20:
                    split_hi(net(3), UP)

            def network(m):
                for h in range(B):
                    for f in range(FT):
                        relu((m, h, f))
                        square(back((m, h, f), 1))
                        if known(m) and m.n == 3 and (h, f) == (0, 3):
                            split_hi(m, DOWN)
                        if not (known(m) and m.n == NN - 1):
                            if (h, f) == (0, 1):
                                split_hi(following(m), UP)
                            if (h, f) == (B - 1, FT - 1):
                                split_hi(following(m), DOWN)

            run_networks(act, network)
            square(BLOCKS[NB - 1])
            for h in range(B):
                act.wait_ge(down_done, NB if h else NB - FT)
                act.activation(y_t[:, h, :], ps[:, Y_BANK[h], :], ACT.Copy).then_inc(y_read, 1)

        @block.vector
        def _(dve):
            steps = [0]

            def step(ins):
                steps[0] += 1
                ins.then_inc(dve_step, 1)

            def link(ins):
                step(ins)
                dve.wait_ge(dve_step, steps[0])

            def layer_norm_stats(which, src, g):
                for t in range(g * TB, (g + 1) * TB):
                    last = dve.bn_stats(stats[:, which, t, :], src[:, t, :])
                link(last)
                for t in range(g * TB, (g + 1) * TB):
                    last = dve.bn_aggr(mv[:, which, t, :], stats[:, which, t, :])
                link(last)
                dve.tensor_scalar(var_eps[:, which, g * TB:(g + 1) * TB], mv[:, which, g * TB:(g + 1) * TB, 1],
                                  EPS, None, ALU.add).then_inc(var_ready, 1)

            def layer_norm_apply(i, which, src, dst, g):
                dve.wait_ge(rstd_ready, i + 1)
                for t in range(g * TB, (g + 1) * TB):
                    dve.tensor_scalar(dst[:, t, :], src[:, t, :], mv[:, which, t, 0:1],
                                      rstd[:, which, t:t + 1], ALU.subtract, ALU.mult).then_inc(xn_ready, 1)

            dve.memset(warm[:, :], 0.0).then_inc(warm_ready, 1)
            dve.wait_ge(head_ready, 1)
            dve.wait_ge(small_in, 16)
            for i in range(3):
                dve.tensor_tensor(bd[:, i, :, :],
                                  small_sb[:, i * HD:(i + 1) * HD].unsqueeze(1).broadcast_to([P, H, HD]),
                                  head_mask[:, :].unsqueeze(2).broadcast_to([P, H, HD]),
                                  ALU.mult).then_inc(bd_ready, 1)
            dve.wait_ge(x_in[0], 16)
            layer_norm_stats(0, x_sb, 0)
            layer_norm_apply(0, 0, x_sb, xn, 0)
            dve.wait_ge(kq_done, 1)
            kq = ps[:, PROB_BANK[1], 0:B * SK].rearrange("p (b k) -> p b k", k=SK)
            dve.tensor_copy(kq_hi[:, :, :], kq).then_inc(kq_split, 1)
            dve.wait_ge(kq_split, 1)
            dve.tensor_tensor(kq_lo[:, :, :], kq, kq_hi[:, :, :].bitcast(F32), ALU.subtract).then_inc(kq_split, 1)

            key_blocks(dve, kblk_hi, kq_hi, 0, 0)
            for t in range(TB):
                dve.wait_ge(xn_hi_done, t + 1)
                dve.tensor_tensor(xn_lo[:, 0, t * P:(t + 1) * P], ps[:, X_BANK[t], 0:P],
                                  xn_hi[:, 0, t * P:(t + 1) * P].bitcast(F32), ALU.subtract).then_inc(xn_lo_done, 1)

            def scores_max(k):
                dve.wait_ge(score_done, k + 1)
                dve.tensor_reduce(s_max[:, k % 2, :].rearrange("p (g j) -> p g j", j=JH),
                                  ps[:, 2 * (k % 2):2 * (k % 2) + 2, 0:JH * SK]
                                  .rearrange("p g (j k) -> p g j k", k=SK), AX_X, ALU.max)\
                    .then_inc(max_done, 1)

            def scores_sub(k):
                dve.wait_ge(max_done, k + 1)
                at_least(dve, exp_done, k - 1)
                dve.tensor_tensor(s_sub[:, k % 2, :, :].rearrange("p (g j) k -> p g j k", j=JH),
                                  ps[:, 2 * (k % 2):2 * (k % 2) + 2, 0:JH * SK]
                                  .rearrange("p g (j k) -> p g j k", k=SK),
                                  s_max[:, k % 2, :].rearrange("p (g j) -> p g j", j=JH).unsqueeze(3)
                                  .broadcast_to([P, 2, JH, SK]), ALU.subtract).then_inc(sub_done, 1)

            def probs_sum(k):
                dve.wait_ge(exp_done, k + 1)
                dve.tensor_reduce(s_sum[:, k % 2, :], prob[:, k % 2, :, :], AX_X, ALU.add).then_inc(sum_done, 1)

            def probs_rec(k):
                dve.wait_ge(sum_done, k + 1)
                at_least(dve, norm_done, k - 1)
                dve.reciprocal(s_rec[:, k % 2, :], s_sum[:, k % 2, :]).then_inc(rec_done, 1)

            def residual(b):
                dve.wait_ge(proj_o, b + 1)
                dve.wait_ge(xbo_ready, 1)
                dve.tensor_tensor(x2[:, b * TB:(b + 1) * TB, :],
                                  ps[:, MISC_BANK, :].rearrange("p (t d) -> p t d", d=D),
                                  x_bo[:, b * TB:(b + 1) * TB, :], ALU.add).then_inc(x2_done, 1)
                dve.wait_ge(x2_done, b + 1)

            for k in range(NU + 1):
                if k == 0:
                    dve.wait_ge(x_in[1], 16)
                    layer_norm_stats(0, x_sb, 1)
                if k < NU:
                    scores_max(k)
                if k > 0:
                    probs_sum(k - 1)
                if k < NU:
                    scores_sub(k)
                if k > 0:
                    probs_rec(k - 1)
                if k == 2:
                    layer_norm_apply(1, 0, x_sb, xn, 1)
                if k == 7:
                    dve.wait_ge(xn_hi_done, TB + 1)
                    dve.tensor_tensor(xn_lo[:, 1, :], ps[:, PV_BANK, :], xn_hi[:, 1, :].bitcast(F32),
                                      ALU.subtract).then_inc(xn_lo_done, 1)
                if k == 16:
                    residual(0)
                    layer_norm_stats(1, x2, 0)
                    layer_norm_apply(2, 1, x2, xn2, 0)

            def router_sub(b):
                dve.wait_ge(logit_done, b + 1)
                logits = ps[:, (MISC_BANK, PV_BANK)[b], 0:TB * NE].rearrange("p (t e) -> p t e", e=NE)
                link(dve.tensor_reduce(r_s[:, 0, :], logits, AX_X, ALU.max))
                dve.tensor_tensor(r_exp[:, b, :, :], logits,
                                  r_s[:, 0, :].unsqueeze(2).broadcast_to([P, TB, NE]), ALU.subtract)\
                    .then_inc(logit_read, 1)

            def over_experts(a):
                return a.unsqueeze(2).broadcast_to([P, TB, NE])

            order = prio[:, :].unsqueeze(1).broadcast_to([P, TB, NE])

            def router_first(b):
                dve.wait_ge(rexp_done, b + 1)
                link(dve.tensor_reduce(r_s[:, 0, :], r_exp[:, b, :, :], AX_X, ALU.add))
                link(dve.reciprocal(r_s[:, 1, :], r_s[:, 0, :]))
                link(dve.tensor_tensor(r_p[:, :, :], r_exp[:, b, :, :], over_experts(r_s[:, 1, :]), ALU.mult))
                link(dve.tensor_reduce(r_s[:, 2, :], r_p[:, :, :], AX_X, ALU.max))
                link(dve.tensor_tensor(r_a[:, :, :], r_p[:, :, :], over_experts(r_s[:, 2, :]), ALU.is_equal))
                link(dve.tensor_tensor(r_a[:, :, :], r_a[:, :, :], order, ALU.mult))
                link(dve.tensor_reduce(r_s[:, 4, :], r_a[:, :, :], AX_X, ALU.max))

            def router_second(b):
                link(dve.tensor_tensor(r_sel[:, b, 0, :, :], r_a[:, :, :], over_experts(r_s[:, 4, :]), ALU.is_equal))
                link(dve.scalar_tensor_tensor(r_a[:, :, :], r_sel[:, b, 0, :, :], -2.0, r_p[:, :, :],
                                              ALU.mult, ALU.add))
                link(dve.tensor_reduce(r_s[:, 3, :], r_a[:, :, :], AX_X, ALU.max))

            def router_weight(b):
                step(dve.tensor_tensor(r_a[:, :, :], r_a[:, :, :], over_experts(r_s[:, 3, :]), ALU.is_equal))
                link(dve.tensor_tensor(r_s[:, 6, :], r_s[:, 2, :], r_s[:, 3, :], ALU.add))
                step(dve.tensor_tensor(r_a[:, :, :], r_a[:, :, :], order, ALU.mult))
                link(dve.tensor_scalar(r_s[:, 6, :], r_s[:, 6, :], 1e-9, None, ALU.max))
                step(dve.tensor_reduce(r_s[:, 5, :], r_a[:, :, :], AX_X, ALU.max))
                link(dve.reciprocal(r_s[:, 7, :], r_s[:, 6, :]))
                step(dve.tensor_tensor(r_sel[:, b, 1, :, :], r_a[:, :, :], over_experts(r_s[:, 5, :]), ALU.is_equal))
                dve.wait_ge(dve_step, steps[0])
                dve.tensor_tensor(r_w[:, b, :, :], r_s[:, 2:4, :],
                                  r_s[:, 7, :].unsqueeze(1).broadcast_to([P, 2, TB]), ALU.mult)\
                   .then_inc(top2_done, 1)

            def hid_high(b):
                i = number(b)
                dve.wait_ge(square_done, i + 1)
                at_least(dve, down_done, i - BPN + 1)
                dve.tensor_copy(hid_hi[:, place(b), :], hid[:, b[2], :]).then_inc(hid_hi_done, 1)

            def hid_low(b):
                dve.wait_ge(hid_hi_done, number(b) + 1)
                dve.tensor_tensor(hid_lo[:, place(b), :], hid[:, b[2], :], hid_hi[:, place(b), :].bitcast(F32),
                                  ALU.subtract).then_inc(hid_lo_done, 1)

            def split_x2(b):
                dve.wait_ge(xn2_read, b + 1)
                dve.tensor_copy(x2_hi[:, b, :], xn2_t[:, b, :]).then_inc(x2_hi_done, 1)
                dve.wait_ge(x2_hi_done, b + 1)
                dve.tensor_tensor(x2_lo[:, b, :], xn2_t[:, b, :], x2_hi[:, b, :].bitcast(F32), ALU.subtract)\
                    .then_inc(x2_lo_done, 1)

            def split_xs(m, h):
                if known(m) and m.n == 1:
                    dve.wait_ge(xs_first_done, h + 1)
                else:
                    dve.wait_ge(xs_done, 2 * (m.n - 2) + h + 1)
                if known(m) and m.n == 2:
                    dve.wait_ge(up_done, number((net(2 * h), 0, FT - 1)) + 1)
                elif known(m) and m.n == 3:
                    dve.wait_ge(up_done, number((net(1), h, FT - 1)) + 1)
                elif not known(m) or m.n > 3:
                    dve.wait_ge(up_done, number((preceding(m), h, FT - 1)) + 1)
                hi, lo = split_input(m, h)
                dve.tensor_copy(hi, xs[:, h, :]).then_inc(xs_hi_done, 1)
                dve.wait_ge(xs_hi_done, xs_number(m, h) + 1)
                dve.tensor_tensor(lo, xs[:, h, :], hi.bitcast(F32), ALU.subtract)\
                    .then_inc(xs_lo_done, 1)

            def scale_x_first(h):
                dve.wait_ge(spread_done, h + 1)
                dve.tensor_tensor(xs[:, h, :], xn2_t[:, h, :], ps[:, SPREAD_BANK[h], :], ALU.mult)\
                    .then_inc(xs_first_done, 1)
                split_xs(net(1), h)

            dve.wait_ge(const_ready, 1)
            router_sub(0)
            router_first(0)
            router_second(0)
            router_weight(0)
            residual(1)

            def hidden(b, prev):
                hid_high(b)
                if prev is not None and not on_pool(prev):
                    hid_low(prev)

            for i in range(EARLY):
                if i == 1:
                    hid_low(BLOCKS[0])
                hidden(BLOCKS[i], BLOCKS[i - 1] if i > 1 else None)
                if i == 1:
                    scale_x_first(0)
                if i == 3:
                    layer_norm_stats(1, x2, 1)
                    layer_norm_apply(3, 1, x2, xn2, 1)
                if i == 4:
                    split_xs(net(2), 0)
                if i == 5:
                    router_sub(1)
                if i == 6:
                    router_first(1)
                    router_second(1)
                if i == 7:
                    split_x2(1)
                    router_weight(1)
                if i == 12:
                    scale_x_first(1)
                if i == 16:
                    split_xs(net(2), 1)
                if i == 19:
                    split_xs(net(3), 0)
                if i == 23:
                    split_xs(net(3), 1)

            def network(m):
                for h in range(B):
                    for f in range(FT):
                        hidden((m, h, f), back((m, h, f), 1))
                        if f == FT - 1 and not (known(m) and m.n == NN - 1):
                            split_xs(following(m), h)

            run_networks(dve, network)
            for h in range(B):
                dve.wait_ge(y_t_done, h + 1)
                dve.tensor_tensor(y_out[:, h * TB:(h + 1) * TB, :],
                                  ps[:, (PV_BANK, MISC_BANK)[h], :].rearrange("p (t d) -> p t d", d=D),
                                  x2[:, h * TB:(h + 1) * TB, :], ALU.add).then_inc(y_ready, 1)

        @block.tensor
        def _(pe):
            def three(out_ap, w, wl, m, ml, start, stop):
                pe.matmul(out_ap, lhsT=w, rhs=m, start=start, stop=False)
                pe.matmul(out_ap, lhsT=w, rhs=ml, start=False, stop=False)
                return pe.matmul(out_ap, lhsT=wl, rhs=m, start=False, stop=stop)

            pe.wait_ge(warm_ready, 1)

            def keep_warm(count):
                for _ in range(count):
                    pe.matmul(ps[:, 3, :], lhsT=warm[:, 0:P], rhs=warm[:, :], start=True, stop=True)

            keep_warm(WARM)

            pe.wait_ge(bd_ready, 3)
            pe.wait_ge(ctx_in, 16)

            def bd_of(i):
                return bd[:, i, :, :].rearrange("p h e -> p (h e)")

            pe.matmul(ps[:, PROB_BANK[0], 0:B * SK], lhsT=bd_of(0), rhs=ctx_sb[:, :], start=True, stop=True)
            pe.matmul(ps[:, PROB_BANK[0], 256:256 + B * SK], lhsT=bd_of(2), rhs=ctx_sb[:, :],
                      start=True, stop=True).then_inc(kv_done, 1)
            pe.wait_ge(kv_read, 1)
            pe.matmul(ps[:, PROB_BANK[1], 0:B * SK], lhsT=bd_of(1), rhs=k_t[:, :],
                      start=True, stop=True).then_inc(kq_done, 1)

            def transpose_x(i, src, g, bank, done):
                for t in range(TB):
                    pe.wait_ge(xn_ready, TB * i + t + 1)
                    pe.transpose(ps[:, bank, t * P:(t + 1) * P], src[:, g * TB + t, :], ident[:, :])\
                        .then_inc(done, 1)

            pe.wait_ge(ident_ready, 1)
            for t in range(TB):
                pe.wait_ge(xn_ready, t + 1)
                if X_BANK[t] == PROB_BANK[0]:
                    pe.wait_ge(kv_read, 2)
                if X_BANK[t] == PROB_BANK[1]:
                    pe.wait_ge(kq_split, 2)
                pe.transpose(ps[:, X_BANK[t], 0:P], xn[:, t, :], ident[:, :]).then_inc(xt_done, 1)
                keep_warm(1 if t < TB - 1 else 3)
            pe.wait_ge(ident_ready, 2)
            pe.wait_ge(bias_ready, 1)

            def scores(k):
                b, half, qt = k // UPB, k % UPB // TB, k % TB
                if k < TB:
                    pe.wait_ge(xn_lo_done, k + 1)
                if qt == 0:
                    pe.wait_ge(kblk_ready[b][half], 2)
                if k == UPB:
                    pe.wait_ge(bias_ready, 2)
                if k == UPB:
                    pe.wait_ge(xn_lo_done, TB + 1)
                at_least(pe, sub_done, k - 1)
                for i in range(2):
                    g = 2 * half + i
                    dst = heads_of(2 * (k % 2) + i)
                    q = slice(qt * P, (qt + 1) * P)
                    pe.matmul(dst, lhsT=ident_bf[:, :],
                              rhs=mask_bias[:, b * TB + qt, :].unsqueeze(1).broadcast_to([P, JH, SK]),
                              start=True, stop=False)
                    heads = slice(g * JH, (g + 1) * JH)
                    last = three(dst, xn_hi[:, b, q], xn_lo[:, b, q],
                                 kblk_hi[:, b, heads, :], kblk_lo[:, b, heads, :], False, True)
                last.then_inc(score_done, 1)

            def transpose_probs(k):
                pe.wait_ge(norm_done, k + 1)
                pe.wait_ge(const_ready, 3)
                at_least(pe, pt_read, 2 * k)
                rows = prob_n[:, k % PNR, :, :].rearrange("p h k -> p (h k)")
                for c in range(CH):
                    i, at = (0, c) if c < 3 else (1, c - 3)
                    ins = pe.transpose(ps[:, PROB_BANK[i], at * P:(at + 1) * P],
                                       rows[:, c * P:(c + 1) * P], ident[:, :])
                    if c in (2, CH - 1):
                        ins.then_inc(pt_done, 1)

            def pv(b, c):
                half = c // CH
                if c % CH == 0:
                    pe.wait_ge(pt_read, 2 * (UPB * b + TB * (half + 1)))
                    if b > 0 and c == 0:
                        pe.wait_ge(attn_read, b)
                pe.wait_ge(vblk_ready, (b * 2 * CH + c) // 4 + 1)
                ins = pe.matmul(ps[:, PV_BANK, :], lhsT=vblk[:, b * 2 * CH + c, :],
                                rhs=prob_t[:, half, c % CH, :], start=(c == 0), stop=(c == 2 * CH - 1))
                if c % CH == CH - 1:
                    ins.then_inc(pv_half, 1)

            def project_out(b):
                pe.wait_ge(attn_read, b + 1)
                if b == 0:
                    pe.wait_ge(wo_in, 16)
                    pe.wait_ge(vblk_ready, 5)
                else:
                    pe.wait_ge(logit_read, b)
                for t in range(TB):
                    last = pe.matmul(ps[:, MISC_BANK, t * P:(t + 1) * P], lhsT=attn_t[:, t * P:(t + 1) * P],
                                     rhs=wo_sb[:, 0:D], start=True, stop=True)
                last.then_inc(proj_o, 1)

            pv_at = {7: (0, (0,)), 8: (0, (1,)), 9: (0, (2,)), 10: (0, (3,)),
                     11: (0, (4, 5)), 12: (0, (6,)), 13: (0, (7,)), 14: (0, (8,)),
                     15: (0, (9,)), 16: (1, (0, 1)), 17: (1, (2, 3)), 18: (1, (4,))}
            for k in range(NU + TLAG):
                if k < NU:
                    scores(k)
                if k == 5:
                    transpose_x(1, xn, 1, PV_BANK, xt_done)
                if 3 <= k < 8:
                    r = k - 3
                    if r == 0:
                        pe.wait_ge(xn_lo_done, TB)
                        pe.wait_ge(vblk_t_ready, 1)
                    if r == 2:
                        pe.wait_ge(vblk_t_ready, 2)
                    at_least(pe, vblk_ready, r)
                    pe.wait_ge(const_ready, 2)
                    flat = vblk_t[:, :, :, :].rearrange("p b h k -> p (b h k)")
                    for j in range(4):
                        c = 4 * r + j
                        last = pe.transpose(ps[:, MISC_BANK, j * P:(j + 1) * P], flat[:, c * P:(c + 1) * P],
                                            ident[:, :])
                    last.then_inc(vt_done, 1)
                if k >= TLAG:
                    transpose_probs(k - TLAG)
                if k == 16:
                    project_out(0)
                if k in pv_at:
                    b, chunks = pv_at[k]
                    if k == 7:
                        pe.wait_ge(xn_lo_done, TB + 1)
                    for c in chunks:
                        pv(b, c)
                if k == 18:
                    pe.wait_ge(x2_done, 1)
                    transpose_x(2, xn2, 0, MISC_BANK, xt2_done)

            def logits(b):
                pe.wait_ge(xn2_read, b + 1)
                if b == 1:
                    pe.wait_ge(root_t_read, 1)
                for t in range(TB):
                    last = pe.matmul(ps[:, (MISC_BANK, PV_BANK)[b], t * NE:(t + 1) * NE], lhsT=xn2_t[:, b, t * P:(t + 1) * P],
                                     rhs=wo_sb[:, D:D + NE], start=True, stop=True)
                last.then_inc(logit_done, 1)

            def transpose_root(b):
                pe.wait_ge(root_done, b + 1)
                if b == 0:
                    pe.wait_ge(attn_read, 2)
                else:
                    pe.wait_ge(xn2_read, 2)
                pe.transpose(ps[0:TB * NE, ROOT_BANK[b], 0:P], root[:, b, :, :].rearrange("p t e -> p (t e)"),
                             ident[:, :]).then_inc(root_t_done, 1)

            def spread_root(b):
                if b == 0:
                    pe.wait_ge(pt_read, 2 * NU)
                else:
                    pe.wait_ge(logit_read, 2)
                pe.wait_ge(root_done, b + 1)
                for t in range(TB):
                    last = pe.transpose(ps[:, SPREAD_BANK[b], t * P:(t + 1) * P],
                                        root[:, b, t, 0:1].broadcast_to([P, P]), ident[:, :])
                last.then_inc(spread_done, 1)

            def up(b):
                m, h, f = b
                i = number(b)
                first = known(m) and m.n == 0
                if isinstance(i, int) and i < FT:
                    pe.wait_ge(sub_done, NU - 1 + f // 2)
                at_least(pe, relu_done, i - FT + 1)
                w_h, w_l = split_weights(m)
                if h == 0 and f == 0:
                    pe.wait_ge(w_lo_done[UP], m.n + 1)
                if f == 0:
                    if first:
                        pe.wait_ge(x2_lo_done, h + 1)
                    else:
                        pe.wait_ge(xs_lo_done, xs_number(m, h) + 1)
                hi, lo = split_input(m, h)
                w = slice(f * P, (f + 1) * P)
                three(ps[:, f, :], w_h[:, w], w_l[:, w], hi, lo, True, True)\
                    .then_inc(up_done, 1)

            def down(b):
                m, h, f = b
                at = place(b)
                w_h, w_l = split_weights(m)
                if known(m) and m.n == 0 and f == 0:
                    if h == 0:
                        pe.wait_ge(pt_read, 2 * NU)
                    else:
                        pe.wait_ge(xs_first_done, 1)
                if h == 0 and f == 0:
                    pe.wait_ge(w_lo_done[DOWN], m.n + 1)
                wait_low(pe, b)
                w = slice(FF + f * P, FF + (f + 1) * P)
                three(ps[:, Y_BANK[h], :], w_h[:, w], w_l[:, w], hid_hi[:, at, :], hid_lo[:, at, :],
                      known(m) and m.n == 0 and f == 0, known(m) and m.n == NN - 1 and f == FT - 1)\
                    .then_inc(down_done, 1)

            pv(1, CH)
            logits(0)
            for c in range(CH + 1, 2 * CH):
                pv(1, c)
            for i in range(EARLY):
                up(BLOCKS[i])
                if i == 1:
                    project_out(1)
                if i == 3:
                    spread_root(0)
                    transpose_root(0)
                    down(BLOCKS[0])
                if i in (4, 5):
                    down(BLOCKS[i - 3])
                if i == 7:
                    pe.wait_ge(x2_done, 2)
                    transpose_x(3, xn2, 1, MISC_BANK, xt2_done)
                    down(BLOCKS[3])
                    logits(1)
                if i >= 10:
                    down(BLOCKS[i - LAG])
                if i == 13:
                    spread_root(1)
                    transpose_root(1)

            def network(m):
                for h in range(B):
                    for f in range(FT):
                        up((m, h, f))
                        down(back((m, h, f), LAG))

            run_networks(pe, network)
            for b in BLOCKS[NB - LAG:]:
                down(b)
            for h in range(B):
                pe.wait_ge(y_read, h + 1)
                bank = (PV_BANK, MISC_BANK)[h]
                for t in range(TB):
                    last = pe.transpose(ps[:, bank, t * P:(t + 1) * P], y_t[:, h, t * P:(t + 1) * P], ident[:, :])
                last.then_inc(y_t_done, 1)


def kernel(x, ctx_1024, mask_Bx1xSxS2_ik1, L0_xattn_Wv, L0_xattn_Wk, L0_xattn_Wq, L0_xattn_Wo, L0_xattn_bo,
           L0_ffn_router_w, L0_ffn_w_fc, L0_ffn_w_proj, L0_ffn_shared_fc, L0_ffn_shared_proj):
    import numpy as np
    import concourse.bacc as bacc
    from concourse.bass_utils import run_bass_kernel_spmd

    up = np.concatenate([np.asarray(L0_ffn_shared_fc)[None], np.asarray(L0_ffn_w_fc)]).transpose(0, 2, 1)
    down = np.concatenate([np.asarray(L0_ffn_shared_proj)[None], np.asarray(L0_ffn_w_proj)])
    down = down.reshape(NN, D, FT, P).transpose(0, 3, 2, 1).reshape(NN, P, FF)
    arrays = {
        "x": np.asarray(x).reshape(B * S, D),
        "ctx_t": np.asarray(ctx_1024).transpose(2, 0, 1).reshape(D, B * SK),
        "mask": np.asarray(mask_Bx1xSxS2_ik1).reshape(B * S, SK),
        "small": np.concatenate([np.asarray(L0_xattn_Wk).T, np.asarray(L0_xattn_Wq), np.asarray(L0_xattn_Wv).T],
                                axis=1),
        "wo_r": np.concatenate([np.asarray(L0_xattn_Wo).T, np.asarray(L0_ffn_router_w).T], axis=1),
        "bo": np.asarray(L0_xattn_bo),
        "w_all": np.concatenate([up, down], axis=2),
    }
    nc = bacc.Bacc("TRN2", target_bir_lowering=False, num_devices=1)
    args = []
    for name, a in arrays.items():
        arrays[name] = a = np.ascontiguousarray(a)
        args.append(nc.dram_tensor(name, a.shape, mybir.dt.from_np(a.dtype), kind="ExternalInput").ap())
    args.append(nc.dram_tensor("out", (B * S, D), F32, kind="ExternalOutput").ap())
    xattn_moe(nc, *args)
    r = run_bass_kernel_spmd(nc, [arrays], core_ids=[0])
    return r.results[0]["out"].reshape(B, S, D)
```

```python
from collections import namedtuple
from contextlib import ExitStack

import concourse.bass as bass
from concourse import mybir

F32 = mybir.dt.float32
F32R = mybir.dt.float32r
BF16 = mybir.dt.bfloat16
I32 = mybir.dt.int32
ALU = mybir.AluOpType
ACT = mybir.ActivationFunctionType
AX_X = mybir.AxisListType.X

P = 128
B, S, D = 2, 512, 128
NT = B * S // P
TB = S // P
H, HD = 16, 8
SK = 77
SKP = 80
UH = H // 2
JH = 4
NU = NT * 2
UPB = TB * 2
CH = UH * SKP // P
NE = 8
NN = NE + 1
FF = 512
FT = FF // P
BPN = B * FT
NB = NN * BPN
LAG = 6
LOOP = (4, 2)
TLAG = 3
PNR = 4
WARM = 9
EPS = 1e-5
MASKED = -1e20
SCALE = 1.0 / float(D) ** 0.5
SMALL = 3 * HD


Net = namedtuple("Net", "n half odd")


def net(n):
    return Net(n, n // 2, n % 2)


def following(m):
    return Net(m.n + 1, m.half + 1 if m.odd else m.half, 1 - m.odd)


def preceding(m):
    return Net(m.n - 1, m.half if m.odd else m.half - 1, 1 - m.odd)


def slot_of(m):
    return 1 - m.odd


def known(m):
    return isinstance(m.n, int)


UNITS = [(n, h) for h in range(B) for n in range(3)] + \
    [(n, h) for n in range(3, NN) for h in range(B)]
BLOCKS = [(net(n), h, f) for n, h in UNITS for f in range(FT)]
EARLY = 3 * BPN
POOL_MORE = (0, 1, 5)


def number(block):
    m, h, f = block
    if known(m):
        return UNITS.index((m.n, h)) * FT + f
    return BPN * m.n + FT * h + f


def back(block, d):
    m, h, f = block
    if known(m):
        return BLOCKS[number(block) - d]
    q = FT * h + f - d
    return (m, q // FT, q % FT) if q >= 0 else (preceding(m), (q + BPN) // FT, (q + BPN) % FT)


def place(block):
    m, h, f = block
    return number(block) % BPN if known(m) else FT * h + f


def on_pool(block):
    m, h, f = block
    return f == FT - 1 or (known(m) and number(block) in POOL_MORE)


def low_count(block):
    m, h, f = block
    if known(m):
        return sum(on_pool(b) == on_pool(block) for b in BLOCKS[:number(block) + 1])
    early = len(POOL_MORE)
    if on_pool(block):
        return early + 2 * m.n + h + 1
    return 3 * (2 * m.n + h) + f + 1 - early


def xs_number(m, h):
    return 2 * h + m.n - 1 if known(m) and m.n < 3 else 2 * (m.n - 1) + h


def xattn_moe(nc, x, ctx_t, mask, small, wo_r, bo, w_all, out):
    ctx = ExitStack()
    with ctx:
        def sb(name, shape, dt):
            return ctx.enter_context(nc.sbuf_tensor(name, shape, dt))

        def sem(name):
            return ctx.enter_context(nc.semaphore(name))

        root_dram = nc.dram_tensor("root_dram", (NE, B * S), F32).ap()

        x_sb = sb("x_sb", [P, NT, D], F32)
        ctx_sb = sb("ctx_sb", [P, B * SK], F32)
        mask_sb = sb("mask_sb", [P, NT, SK], I32)
        small_sb = sb("small_sb", [P, SMALL], F32)
        wo_sb = sb("wo_sb", [P, D + NE], F32)
        bo_sb = sb("bo_sb", [P, D], F32)
        ident = sb("ident", [P, P], F32)
        ident_bf = sb("ident_bf", [P, P], BF16)
        head_mask = sb("head_mask", [P, H], F32)
        warm = sb("warm", [P, 512], BF16)
        minus_half = sb("minus_half", [P, TB], F32)
        prio = sb("prio", [P, NE], F32)
        stats = sb("stats", [P, 2, NT, 6], F32)
        mv = sb("mv", [P, 2, NT, 2], F32)
        var_eps = sb("var_eps", [P, 2, NT], F32)
        rstd = sb("rstd", [P, 2, NT], F32)
        xn = sb("xn", [P, NT, D], F32)
        xn_hi = sb("xn_hi", [P, B, S], F32R)
        xn_lo = sb("xn_lo", [P, B, S], F32R)
        shared = sb("shared", [P, 2 * BPN * S], F32R)
        kb = B * H * SK
        kblk_hi = shared[:, 0:kb].rearrange("p (b h k) -> p b h k", b=B, h=H)
        kblk_lo = shared[:, kb:2 * kb].rearrange("p (b h k) -> p b h k", b=B, h=H)
        hid_hi = shared[:, 0:BPN * S].rearrange("p (i s) -> p i s", i=BPN)
        hid_lo = shared[:, BPN * S:2 * BPN * S].rearrange("p (i s) -> p i s", i=BPN)
        bd = sb("bd", [P, 3, H, HD], F32)
        k_t = sb("k_t", [P, B * SK], F32)
        v_t = sb("v_t", [P, B, SK], F32)
        vblk_t = sb("vblk_t", [P, B, H, SKP], F32)
        kq_hi = sb("kq_hi", [P, B, SK], F32R)
        kq_lo = sb("kq_lo", [P, B, SK], F32R)
        vblk = sb("vblk", [P, B * 2 * CH, P], F32)
        mask_bias = sb("mask_bias", [P, NT, SK], BF16)
        s_max = sb("s_max", [P, 2, UH], F32)
        s_sum = sb("s_sum", [P, 2, UH], F32)
        s_rec = sb("s_rec", [P, 2, UH], F32)
        s_sub = sb("s_sub", [P, 2, UH, SK], F32)
        prob = sb("prob", [P, 2, UH, SK], F32)
        prob_n = sb("prob_n", [P, PNR, UH, SKP], F32)
        prob_t = sb("prob_t", [P, 2, CH, S], F32)
        attn_t = sb("attn_t", [P, S], F32)
        x_bo = sb("x_bo", [P, NT, D], F32)
        x2 = sb("x2", [P, NT, D], F32)
        xn2 = sb("xn2", [P, NT, D], F32)
        xn2_t = sb("xn2_t", [P, B, S], F32)
        x2_hi = sb("x2_hi", [P, B, S], F32R)
        x2_lo = sb("x2_lo", [P, B, S], F32R)
        r_exp = sb("r_exp", [P, B, TB, NE], F32)
        r_p = sb("r_p", [P, TB, NE], F32)
        r_a = sb("r_a", [P, TB, NE], F32)
        r_s = sb("r_s", [P, 8, TB], F32)
        r_sel = sb("r_sel", [P, B, 2, TB, NE], F32)
        r_w = sb("r_w", [P, B, 2, TB], F32)
        r_term = sb("r_term", [P, 2, TB, NE], F32)
        half = sb("half", [P, 2, TB], F32)
        root = sb("root", [P, B, TB, NE], F32)
        root_t = sb("root_t", [TB * NE, B, P], F32)
        w_raw = sb("w_raw", [P, 2, 2 * FF], F32)
        w_hi = sb("w_hi", [P, 2, 2 * FF], F32R)
        w_lo = sb("w_lo", [P, 2, 2 * FF], F32R)
        w_hi_2 = xn_hi[:, :, :].rearrange("p b s -> p (b s)")
        w_lo_2 = xn_lo[:, :, :].rearrange("p b s -> p (b s)")
        root_b = sb("root_b", [P, 2, B, S], F32)
        xs = sb("xs", [P, B, S], F32)
        xs_hi = sb("xs_hi", [P, B, S], F32R)
        xs_lo = sb("xs_lo", [P, B, S], F32R)
        hid_r = sb("hid_r", [P, 2, S], F32)
        hid = sb("hid", [P, FT, S], F32)
        y_t = prob_t[:, 0, 0:B, :]
        y_out = xn

        ps = ctx.enter_context(nc.psum_tensor("ps", [P, 8, 512], F32))
        PROB_BANK = (4, 5)
        Y_BANK = (4, 5)
        PV_BANK, MISC_BANK = 6, 7
        OUT_BANK = (6, 7, 6, 7)
        LOGIT_BANK = (7, 6)
        ROOT_BANK = (6, 7)
        SPREAD_BANK = (5, 6)
        X_BANK = (6, 7, 4, 5)

        x_in = [sem("x_in0"), sem("x_in1")]
        mask_in = [sem("mask_in0"), sem("mask_in1")]
        ctx_in, small_in, wo_in, bo_in = (sem(n) for n in ("ctx_in", "small_in", "wo_in", "bo_in"))
        w_in = [[sem(f"w_in{q}{part}") for part in ("up", "down")] for q in range(2)]
        root_in = [[sem(f"root_in{q}{h}") for h in range(B)] for q in range(2)]
        root_out = [sem("root_out0"), sem("root_out1")]
        out_done = sem("out_done")
        pool_step, dve_step = sem("pool_step"), sem("dve_step")
        ident_ready, const_ready, bd_ready, head_ready = (sem(n) for n in (
            "ident_ready", "const_ready", "bd_ready", "head_ready"))
        bias_ready, xbo_ready, vblk_t_ready = sem("bias_ready"), sem("xbo_ready"), sem("vblk_t_ready")
        var_ready, rstd_ready, xn_ready = sem("var_ready"), sem("rstd_ready"), sem("xn_ready")
        xt_done, xn_hi_done, xn_lo_done = sem("xt_done"), sem("xn_hi_done"), sem("xn_lo_done")
        kv_done, kv_read, kq_done, kq_split, warm_ready = (sem(n) for n in (
            "kv_done", "kv_read", "kq_done", "kq_split", "warm_ready"))
        kblk_ready = [[sem(f"kblk_ready{b}{half}") for half in range(2)] for b in range(B)]
        vt_done, vblk_ready = sem("vt_done"), sem("vblk_ready")
        score_done, max_done, sub_done, exp_done, sum_done, rec_done, norm_done = (sem(n) for n in (
            "score_done", "max_done", "sub_done", "exp_done", "sum_done", "rec_done", "norm_done"))
        pt_done, pt_read, pv_done, attn_read, proj_o = (sem(n) for n in (
            "pt_done", "pt_read", "pv_done", "attn_read", "proj_o"))
        x2_done, xt2_done, xn2_read, x2_hi_done, x2_lo_done = (sem(n) for n in (
            "x2_done", "xt2_done", "xn2_read", "x2_hi_done", "x2_lo_done"))
        logit_done, logit_read, rexp_done, top2_done, root_done, root_t_done, root_t_read = (
            sem(n) for n in ("logit_done", "logit_read", "rexp_done", "top2_done", "root_done",
                             "root_t_done", "root_t_read"))
        spread_done = sem("spread_done")
        w_hi_done = [sem("w_hi_done_up"), sem("w_hi_done_down")]
        w_lo_done = [sem("w_lo_done_up"), sem("w_lo_done_down")]
        xs_first_done, xs_second_done = sem("xs_first_done"), sem("xs_second_done")
        xs_done, xs_hi_done, xs_lo_done = sem("xs_done"), sem("xs_hi_done"), sem("xs_lo_done")
        hid_lo_pool_done = sem("hid_lo_pool_done")
        up_done, relu_done, square_done, hid_hi_done, hid_lo_done, down_done = (sem(n) for n in (
            "up_done", "relu_done", "square_done", "hid_hi_done", "hid_lo_done", "down_done"))
        y_read, y_t_done, y_ready = sem("y_read"), sem("y_t_done"), sem("y_ready")

        def at_least(eng, s, n):
            if not isinstance(n, int) or n > 0:
                eng.wait_ge(s, n)

        def heads_of(bank):
            return ps[:, bank, 0:JH * SK].rearrange("p (j k) -> p j k", k=SK)

        def wait_low(eng, b):
            eng.wait_ge(hid_lo_pool_done if on_pool(b) else hid_lo_done, low_count(b))

        def part_of(part):
            return slice(part * FF, (part + 1) * FF)

        UP, DOWN = 0, 1

        def split_weights(m):
            if known(m) and m.n == 2:
                return w_hi_2, w_lo_2
            return w_hi[:, slot_of(m), :], w_lo[:, slot_of(m), :]

        def split_input(m, h):
            if known(m) and m.n in (0, 2):
                at = h if m.n == 0 else 0
                return x2_hi[:, at, :], x2_lo[:, at, :]
            return xs_hi[:, h, :], xs_lo[:, h, :]

        def run_networks(eng, network):
            first, pairs = LOOP
            for n in range(3, first):
                network(net(n))
            with eng.Fori(0, pairs) as k:
                network(Net(2 * k + first, k + first // 2, 0))
                network(Net(2 * k + first + 1, k + first // 2, 1))
            for n in range(first + 2 * pairs, NN):
                network(net(n))

        def key_blocks(eng, dst, src, b, half):
            heads = slice(half * UH, half * UH + UH)
            eng.wait_ge(kq_split, 2)
            eng.tensor_tensor(dst[:, b, heads, :],
                              src[:, b, :].bitcast(F32).unsqueeze(1).broadcast_to([P, UH, SK]),
                              head_mask[:, heads].unsqueeze(2).broadcast_to([P, UH, SK]), ALU.mult)\
               .then_inc(kblk_ready[b][half], 1)

        def scale_x(eng, m, h):
            eng.wait_ge(root_in[slot_of(m)][h], 16 * m.half)
            eng.wait_ge(xs_lo_done, xs_number(preceding(m), h) + 1)
            eng.tensor_tensor(xs[:, h, :], xn2_t[:, h, :], root_b[:, slot_of(m), h, :], ALU.mult)\
               .then_inc(xs_second_done if known(m) and m.n == 2 else xs_done, 1)

        block = ctx.enter_context(nc.Block())

        @block.sync
        def _(sp):
            x_v = x.rearrange("(t p) d -> p t d", p=P)
            sp.dma_start(x_sb[:, 0:TB, :], x_v[:, 0:TB, :]).then_inc(x_in[0], 16)
            sp.dma_start(ctx_sb[:, :], ctx_t).then_inc(ctx_in, 16)
            mask_v = mask.rearrange("(t p) k -> p t k", p=P)
            for b in range(B):
                sp.dma_start(mask_sb[:, b * TB:(b + 1) * TB, :], mask_v[:, b * TB:(b + 1) * TB, :])\
                  .then_inc(mask_in[b], 16)
            sp.dma_start(x_sb[:, TB:NT, :], x_v[:, TB:NT, :]).then_inc(x_in[1], 16)
            sp.dma_start(wo_sb[:, :], wo_r).then_inc(wo_in, 16)
            sp.dma_start(bo_sb[:, :], bo.partition_broadcast(P)).then_inc(bo_in, 16)

            def load_w(m, part):
                slot = slot_of(m)
                at_least(sp, w_lo_done[part], m.n - 1)
                src = w_all[bass.ds(m.n, 1), :, part_of(part)].rearrange("n p c -> p (n c)")
                sp.dma_start(w_raw[:, slot, part_of(part)], src)\
                  .then_inc(w_in[slot][part], 16)

            def load_root(m, h):
                slot = slot_of(m)
                if known(m) and m.n == 4:
                    sp.wait_ge(xs_second_done, h + 1)
                elif not known(m) or m.n > 4:
                    sp.wait_ge(xs_done, 2 * (m.n - 5) + h + 1)
                row = root_dram[bass.ds(m.n - 1, 1), h * S:(h + 1) * S].rearrange("e s -> (e s)")
                sp.dma_start(root_b[:, slot, h, :], row.partition_broadcast(P))\
                  .then_inc(root_in[slot][h], 16)

            for n in range(4):
                load_w(net(n), UP)
                load_w(net(n), DOWN)
            for h in range(B):
                sp.wait_ge(root_t_read, h + 1)
                sp.dma_start(root_dram.rearrange("e (b t p) -> b t e p", b=B, t=TB)[h, :, :, :],
                             root_t[:, h, :]).then_inc(root_out[h], 16)
                sp.wait_ge(root_out[h], 16)
                for n in (2, 3):
                    load_root(net(n), h)

            def network(m):
                if known(m) and m.n == NN - 1:
                    return
                load_w(following(m), UP)
                for h in range(B):
                    load_root(following(m), h)
                load_w(following(m), DOWN)

            run_networks(sp, network)
            out_v = out.rearrange("(t p) d -> p t d", p=P)
            for i in range(2 * B):
                tiles = slice(i * TB // 2, (i + 1) * TB // 2)
                sp.wait_ge(y_ready, i + 1)
                sp.dma_start(out_v[:, tiles, :], y_out[:, tiles, :]).then_inc(out_done, 16)
            sp.wait_ge(out_done, 16 * 2 * B)

        @block.gpsimd
        def _(pool):
            steps = [0]

            def link(ins):
                steps[0] += 1
                ins.then_inc(pool_step, 1)
                pool.wait_ge(pool_step, steps[0])

            link(pool.memset(head_mask[:, :], 1.0))
            link(pool.affine_select(out=head_mask[:, :], in_=head_mask[:, :], compare_op=ALU.is_ge, fill=0.0,
                                    base=0, pattern=[[-HD, H]], channel_multiplier=1))
            pool.affine_select(out=head_mask[:, :], in_=head_mask[:, :], compare_op=ALU.is_ge, fill=0.0,
                               base=HD - 1, pattern=[[HD, H]], channel_multiplier=-1).then_inc(head_ready, 1)
            link(pool.memset(ident[:, :], 0.0))
            pool.affine_select(out=ident[:, :], in_=ident[:, :], compare_op=ALU.not_equal, fill=1.0,
                               base=0, pattern=[[-1, P]], channel_multiplier=1).then_inc(ident_ready, 1)
            pool.memset(half[:, :, :], 0.5)
            link(pool.memset(minus_half[:, :], -0.5))

            def root_inverse(i, which, g):
                pool.wait_ge(var_ready, i + 1)
                pool.tensor_tensor(rstd[:, which, g * TB:(g + 1) * TB], var_eps[:, which, g * TB:(g + 1) * TB],
                                   minus_half[:, :], ALU.pow).then_inc(rstd_ready, 1)

            def mask_to_bias(first, last):
                pool.wait_ge(mask_in[first // TB], 16)
                pool.tensor_scalar(mask_bias[:, first:last, :], mask_sb[:, first:last, :],
                                   0.0, MASKED, ALU.is_equal, ALU.mult).then_inc(bias_ready, 1)

            pool.wait_ge(ident_ready, 1)
            pool.tensor_copy(ident_bf[:, :], ident[:, :]).then_inc(ident_ready, 1)
            root_inverse(0, 0, 0)
            mask_to_bias(0, 1)
            key_blocks(pool, kblk_lo, kq_lo, 0, 0)
            mask_to_bias(1, TB)
            for i in range(NE):
                last = pool.memset(prio[:, i:i + 1], float(NE - i))
            last.then_inc(const_ready, 1)
            pool.memset(vblk_t[:, :, :, SK:SKP], 0.0).then_inc(const_ready, 1)
            pool.memset(prob_n[:, :, :, SK:SKP], 0.0).then_inc(const_ready, 1)
            root_inverse(1, 0, 1)

            def normalise(k):
                pool.wait_ge(rec_done, k + 1)
                at_least(pool, pt_done, 2 * (k - PNR + 1))
                pool.tensor_tensor(prob_n[:, k % PNR, :, 0:SK], prob[:, k % 2, :, :],
                                   s_rec[:, k % 2, :].unsqueeze(2).broadcast_to([P, UH, SK]),
                                   ALU.mult).then_inc(norm_done, 1)

            def add_bias(b):
                pool.wait_ge(bo_in, 16)
                pool.wait_ge(x_in[b], 16)
                tiles = slice(b * TB, (b + 1) * TB)
                pool.tensor_tensor(x_bo[:, tiles, :], x_sb[:, tiles, :],
                                   bo_sb[:, :].unsqueeze(1).broadcast_to([P, TB, D]), ALU.add)\
                    .then_inc(xbo_ready, 1)

            def v_blocks(b):
                pool.wait_ge(kv_read, 2)
                pool.tensor_tensor(vblk_t[:, b, :, 0:SK], v_t[:, b, :].unsqueeze(1).broadcast_to([P, H, SK]),
                                   head_mask[:, :].unsqueeze(2).broadcast_to([P, H, SK]),
                                   ALU.mult).then_inc(vblk_t_ready, 1)

            def split_lo(m, part):
                at = part_of(part)
                hi, lo = split_weights(m)
                pool.wait_ge(w_hi_done[part], m.n + 1)
                pool.tensor_tensor(lo[:, at], w_raw[:, slot_of(m), at], hi[:, at].bitcast(F32),
                                   ALU.subtract).then_inc(w_lo_done[part], 1)

            v_blocks(0)
            for k in range(NU):
                if k == NU - 1:
                    root_inverse(2, 1, 0)
                normalise(k)
                if k == 4:
                    mask_to_bias(TB, NT)
                if k in (3, 8):
                    key_blocks(pool, kblk_lo, kq_lo, 1, k // 8)
                if k == 0:
                    v_blocks(1)
                if k == 12:
                    add_bias(0)
                if k == NU - 1:
                    add_bias(1)
                if k in (8, 9, 10, 11):
                    split_lo(net((k - 8) // 2), k % 2)

            def roots(b):
                pool.wait_ge(top2_done, b + 1)
                link(pool.tensor_tensor(r_w[:, b, :, :], r_w[:, b, :, :], half[:, :, :], ALU.pow))
                link(pool.tensor_tensor(r_term[:, :, :, :], r_sel[:, b, :, :, :],
                                        r_w[:, b, :, :].unsqueeze(3).broadcast_to([P, 2, TB, NE]), ALU.mult))
                pool.tensor_tensor(root[:, b, :, :], r_term[:, 0, :, :], r_term[:, 1, :, :], ALU.add)\
                    .then_inc(root_done, 1)
                pool.wait_ge(root_done, b + 1)

            def hid_low(b):
                pool.wait_ge(hid_hi_done, number(b) + 1)
                pool.tensor_tensor(hid_lo[:, place(b), :], hid[:, b[2], :], hid_hi[:, place(b), :].bitcast(F32),
                                   ALU.subtract).then_inc(hid_lo_pool_done, 1)

            def x2_low(b):
                pool.wait_ge(x2_hi_done, b + 1)
                pool.tensor_tensor(x2_lo[:, b, :], xn2_t[:, b, :], x2_hi[:, b, :].bitcast(F32), ALU.subtract)\
                    .then_inc(x2_lo_done, 1)

            x2_low(0)
            split_lo(net(2), UP)
            split_lo(net(2), DOWN)
            roots(0)
            hid_low(BLOCKS[0])
            for i in range(1, EARLY - 1):
                if on_pool(BLOCKS[i]):
                    hid_low(BLOCKS[i])
                if i == 3:
                    root_inverse(3, 1, 1)
                if i == 5:
                    x2_low(1)
                if i == 7:
                    roots(1)
                if i == 15:
                    scale_x(pool, net(3), 0)
                if i == 18:
                    split_lo(net(3), UP)
            scale_x(pool, net(3), 1)

            def network(m):
                last = known(m) and m.n == NN - 1
                early = known(m) and m.n == 3
                if not last:
                    scale_x(pool, following(m), 0)
                if not early:
                    split_lo(m, DOWN)
                hid_low(back((m, 0, 0), 1))
                if early:
                    split_lo(m, DOWN)
                if not last:
                    split_lo(following(m), UP)
                    scale_x(pool, following(m), 1)
                hid_low((m, 0, FT - 1))

            run_networks(pool, network)
            hid_low(BLOCKS[NB - 1])

        @block.scalar
        def _(act):
            act.dma_start(small_sb[:, :],
                          bass.AP(tensor=small.tensor, offset=0, ap=[[0, H], [SMALL, HD], [1, SMALL]]))\
                .then_inc(small_in, 16)

            act.wait_ge(kv_done, 1)
            act.activation(k_t[:, :], ps[:, PROB_BANK[0], 0:B * SK], ACT.Copy).then_inc(kv_read, 1)
            act.activation(v_t[:, :, :].rearrange("p b k -> p (b k)"),
                           ps[:, PROB_BANK[0], 256:256 + B * SK], ACT.Copy).then_inc(kv_read, 1)

            act.wait_ge(kq_done, 1)
            act.activation(kq_hi[:, :, :], ps[:, PROB_BANK[1], 0:B * SK].rearrange("p (b k) -> p b k", k=SK),
                           ACT.Copy).then_inc(kq_split, 1)

            for t in range(TB):
                act.wait_ge(xt_done, t + 1)
                act.activation(xn_hi[:, 0, t * P:(t + 1) * P], ps[:, X_BANK[t], 0:P], ACT.Copy)\
                    .then_inc(xn_hi_done, 1)

            def spread_keys(dst, src, b, half):
                act.wait_ge(kq_split, 2)
                for head in range(half * UH, half * UH + UH):
                    last = act.activation(dst[:, b, head, :], src[:, b, :].bitcast(F32), ACT.Copy,
                                          scale=head_mask[:, head:head + 1])
                last.then_inc(kblk_ready[b][half], 1)

            spread_keys(kblk_hi, kq_hi, 0, 1)
            spread_keys(kblk_lo, kq_lo, 0, 1)

            def exps(k):
                act.wait_ge(sub_done, k + 1)
                at_least(act, norm_done, k - 1)
                act.activation(prob[:, k % 2, :, :], s_sub[:, k % 2, :, :], ACT.Exp, scale=SCALE)\
                    .then_inc(exp_done, 1)

            def read_transposed(k):
                b, half, qt = k // UPB, k % UPB // TB, k % TB
                if b > 0:
                    act.wait_ge(pv_done, half + 1)
                at = 0
                for i, cnt in enumerate((3, CH - 3)):
                    act.wait_ge(pt_done, 2 * k + i + 1)
                    act.activation(prob_t[:, half, at:at + cnt, qt * P:(qt + 1) * P],
                                   ps[:, PROB_BANK[i], 0:cnt * P].rearrange("p (c q) -> p c q", q=P),
                                   ACT.Copy).then_inc(pt_read, 1)
                    at += cnt

            def read_attn(b):
                act.wait_ge(pv_done, 2 * b + 2)
                if b > 0:
                    act.wait_ge(proj_o, b)
                act.activation(attn_t[:, :], ps[:, PV_BANK, :], ACT.Copy).then_inc(attn_read, 1)

            def read_xn2(b):
                act.wait_ge(xt2_done, TB * (b + 1))
                act.activation(xn2_t[:, b, :], ps[:, MISC_BANK, :], ACT.Copy).then_inc(xn2_read, 1)

            def x2_high(b):
                act.wait_ge(xn2_read, b + 1)
                act.activation(x2_hi[:, b, :], xn2_t[:, b, :], ACT.Copy).then_inc(x2_hi_done, 1)

            def split_hi(m, part):
                slot, at = slot_of(m), part_of(part)
                act.wait_ge(w_in[slot][part], 16 * (m.half + 1))
                if known(m) and m.n == 2:
                    act.wait_ge(score_done, NU)
                elif not known(m) or m.n > 2:
                    before = preceding(preceding(m))
                    act.wait_ge((up_done, down_done)[part], number((before, B - 1, FT - 1)) + 1)
                act.activation(split_weights(m)[0][:, at], w_raw[:, slot, at], ACT.Copy)\
                    .then_inc(w_hi_done[part], 1)

            def router_exp(b):
                act.wait_ge(logit_read, b + 1)
                act.activation(r_exp[:, b, :, :], r_exp[:, b, :, :], ACT.Exp).then_inc(rexp_done, 1)

            for k in range(NU + TLAG):
                if k == NU + TLAG - 1:
                    read_xn2(0)
                if k == 15:
                    read_attn(0)
                if k >= TLAG:
                    read_transposed(k - TLAG)
                if 4 <= k < 9:
                    r = k - 4
                    act.wait_ge(vt_done, r + 1)
                    act.activation(vblk[:, 4 * r:4 * r + 4, :],
                                   ps[:, MISC_BANK, :].rearrange("p (c q) -> p c q", q=P), ACT.Copy)\
                        .then_inc(vblk_ready, 1)
                if k < NU:
                    exps(k)
                if k in (0, 1):
                    spread_keys(kblk_hi, kq_hi, 1, k)
                if k == 5:
                    act.wait_ge(xt_done, NT)
                    act.activation(xn_hi[:, 1, :], ps[:, PV_BANK, :], ACT.Copy).then_inc(xn_hi_done, 1)
                if k in (8, 9, 10, 11):
                    split_hi(net((k - 8) // 2), k % 2)
                if k in (16, 17):
                    split_hi(net(2), k % 2)
            x2_high(0)

            def relu(b):
                i, f = number(b), b[2]
                act.wait_ge(up_done, i + 1)
                at_least(act, square_done, i - 1)
                act.activation(hid_r[:, f % 2, :], ps[:, f, :], ACT.Relu).then_inc(relu_done, 1)

            def square(b):
                i, f = number(b), b[2]
                act.wait_ge(relu_done, i + 1)
                if not isinstance(i, int) or i >= FT:
                    wait_low(act, back(b, FT))
                act.activation(hid[:, f, :], hid_r[:, f % 2, :], ACT.Square).then_inc(square_done, 1)

            def read_root(b):
                act.wait_ge(root_t_done, b + 1)
                act.activation(root_t[:, b, :], ps[0:TB * NE, ROOT_BANK[b], 0:P], ACT.Copy).then_inc(root_t_read, 1)

            router_exp(0)
            read_attn(1)
            for i in range(EARLY):
                if i == FT - 1:
                    read_root(0)
                relu(BLOCKS[i])
                if i not in (0, FT):
                    square(BLOCKS[i - 1])
                if i == FT - 1:
                    square(BLOCKS[i])
                if i == 7:
                    read_xn2(1)
                if i == 8:
                    router_exp(1)
                    x2_high(1)
                if i == 14:
                    read_root(1)
                if i == 19:
                    split_hi(net(3), UP)

            def network(m):
                for h in range(B):
                    for f in range(FT):
                        relu((m, h, f))
                        square(back((m, h, f), 1))
                        if known(m) and m.n == 3 and (h, f) == (0, 3):
                            split_hi(m, DOWN)
                        if not (known(m) and m.n == NN - 1):
                            if (h, f) == (0, 1):
                                split_hi(following(m), UP)
                            if (h, f) == (B - 1, FT - 1):
                                split_hi(following(m), DOWN)

            run_networks(act, network)
            square(BLOCKS[NB - 1])
            for i in range(2 * B):
                h, tokens = i // 2, slice(i % 2 * S // 2, (i % 2 + 1) * S // 2)
                act.wait_ge(down_done, NB if h else NB - FT)
                act.activation(y_t[:, h, tokens], ps[:, Y_BANK[h], tokens], ACT.Copy).then_inc(y_read, 1)

        @block.vector
        def _(dve):
            steps = [0]

            def step(ins):
                steps[0] += 1
                ins.then_inc(dve_step, 1)

            def link(ins):
                step(ins)
                dve.wait_ge(dve_step, steps[0])

            def layer_norm_stats(which, src, g):
                for t in range(g * TB, (g + 1) * TB):
                    last = dve.bn_stats(stats[:, which, t, :], src[:, t, :])
                link(last)
                for t in range(g * TB, (g + 1) * TB):
                    last = dve.bn_aggr(mv[:, which, t, :], stats[:, which, t, :])
                link(last)
                dve.tensor_scalar(var_eps[:, which, g * TB:(g + 1) * TB], mv[:, which, g * TB:(g + 1) * TB, 1],
                                  EPS, None, ALU.add).then_inc(var_ready, 1)

            def layer_norm_apply(i, which, src, dst, g):
                dve.wait_ge(rstd_ready, i + 1)
                for t in range(g * TB, (g + 1) * TB):
                    dve.tensor_scalar(dst[:, t, :], src[:, t, :], mv[:, which, t, 0:1],
                                      rstd[:, which, t:t + 1], ALU.subtract, ALU.mult).then_inc(xn_ready, 1)

            dve.memset(warm[:, :], 0.0).then_inc(warm_ready, 1)
            dve.wait_ge(head_ready, 1)
            dve.wait_ge(small_in, 16)
            for i in range(3):
                dve.tensor_tensor(bd[:, i, :, :],
                                  small_sb[:, i * HD:(i + 1) * HD].unsqueeze(1).broadcast_to([P, H, HD]),
                                  head_mask[:, :].unsqueeze(2).broadcast_to([P, H, HD]),
                                  ALU.mult).then_inc(bd_ready, 1)
            dve.wait_ge(x_in[0], 16)
            layer_norm_stats(0, x_sb, 0)
            layer_norm_apply(0, 0, x_sb, xn, 0)
            kq = ps[:, PROB_BANK[1], 0:B * SK].rearrange("p (b k) -> p b k", k=SK)
            dve.wait_ge(kq_split, 1)
            dve.tensor_tensor(kq_lo[:, :, :], kq, kq_hi[:, :, :].bitcast(F32), ALU.subtract).then_inc(kq_split, 1)

            key_blocks(dve, kblk_hi, kq_hi, 0, 0)
            for t in range(TB):
                dve.wait_ge(xn_hi_done, t + 1)
                dve.tensor_tensor(xn_lo[:, 0, t * P:(t + 1) * P], ps[:, X_BANK[t], 0:P],
                                  xn_hi[:, 0, t * P:(t + 1) * P].bitcast(F32), ALU.subtract).then_inc(xn_lo_done, 1)

            def scores_max(k):
                dve.wait_ge(score_done, k + 1)
                dve.tensor_reduce(s_max[:, k % 2, :].rearrange("p (g j) -> p g j", j=JH),
                                  ps[:, 2 * (k % 2):2 * (k % 2) + 2, 0:JH * SK]
                                  .rearrange("p g (j k) -> p g j k", k=SK), AX_X, ALU.max)\
                    .then_inc(max_done, 1)

            def scores_sub(k):
                dve.wait_ge(max_done, k + 1)
                at_least(dve, exp_done, k - 1)
                dve.tensor_tensor(s_sub[:, k % 2, :, :].rearrange("p (g j) k -> p g j k", j=JH),
                                  ps[:, 2 * (k % 2):2 * (k % 2) + 2, 0:JH * SK]
                                  .rearrange("p g (j k) -> p g j k", k=SK),
                                  s_max[:, k % 2, :].rearrange("p (g j) -> p g j", j=JH).unsqueeze(3)
                                  .broadcast_to([P, 2, JH, SK]), ALU.subtract).then_inc(sub_done, 1)

            def probs_sum(k):
                dve.wait_ge(exp_done, k + 1)
                dve.tensor_reduce(s_sum[:, k % 2, :], prob[:, k % 2, :, :], AX_X, ALU.add).then_inc(sum_done, 1)

            def probs_rec(k):
                dve.wait_ge(sum_done, k + 1)
                at_least(dve, norm_done, k - 1)
                dve.reciprocal(s_rec[:, k % 2, :], s_sum[:, k % 2, :]).then_inc(rec_done, 1)

            def residual(b):
                dve.wait_ge(proj_o, b + 1)
                dve.wait_ge(xbo_ready, b + 1)
                dve.tensor_tensor(x2[:, b * TB:(b + 1) * TB, :],
                                  ps[:, MISC_BANK, :].rearrange("p (t d) -> p t d", d=D),
                                  x_bo[:, b * TB:(b + 1) * TB, :], ALU.add).then_inc(x2_done, 1)
                dve.wait_ge(x2_done, b + 1)

            for k in range(NU + 1):
                if k == 0:
                    dve.wait_ge(x_in[1], 16)
                    layer_norm_stats(0, x_sb, 1)
                if k < NU:
                    scores_max(k)
                if k == NU:
                    residual(0)
                    layer_norm_stats(1, x2, 0)
                if k > 0:
                    probs_sum(k - 1)
                if k < NU:
                    scores_sub(k)
                if k > 0:
                    probs_rec(k - 1)
                if k == 2:
                    layer_norm_apply(1, 0, x_sb, xn, 1)
                if k == 6:
                    dve.wait_ge(xn_hi_done, TB + 1)
                    dve.tensor_tensor(xn_lo[:, 1, :], ps[:, PV_BANK, :], xn_hi[:, 1, :].bitcast(F32),
                                      ALU.subtract).then_inc(xn_lo_done, 1)
            layer_norm_apply(2, 1, x2, xn2, 0)

            def router_sub(b):
                dve.wait_ge(logit_done, b + 1)
                logits = ps[:, LOGIT_BANK[b], 0:TB * NE].rearrange("p (t e) -> p t e", e=NE)
                link(dve.tensor_reduce(r_s[:, 0, :], logits, AX_X, ALU.max))
                dve.tensor_tensor(r_exp[:, b, :, :], logits,
                                  r_s[:, 0, :].unsqueeze(2).broadcast_to([P, TB, NE]), ALU.subtract)\
                    .then_inc(logit_read, 1)

            def over_experts(a):
                return a.unsqueeze(2).broadcast_to([P, TB, NE])

            order = prio[:, :].unsqueeze(1).broadcast_to([P, TB, NE])

            def router_first(b):
                dve.wait_ge(rexp_done, b + 1)
                link(dve.tensor_reduce(r_s[:, 0, :], r_exp[:, b, :, :], AX_X, ALU.add))
                step(dve.tensor_reduce(r_s[:, 5, :], r_exp[:, b, :, :], AX_X, ALU.max))
                link(dve.reciprocal(r_s[:, 1, :], r_s[:, 0, :]))
                step(dve.tensor_tensor(r_p[:, :, :], r_exp[:, b, :, :], over_experts(r_s[:, 1, :]), ALU.mult))
                link(dve.tensor_tensor(r_s[:, 2, :], r_s[:, 5, :], r_s[:, 1, :], ALU.mult))
                link(dve.tensor_tensor(r_a[:, :, :], r_p[:, :, :], over_experts(r_s[:, 2, :]), ALU.is_equal))
                link(dve.tensor_tensor(r_a[:, :, :], r_a[:, :, :], order, ALU.mult))
                link(dve.tensor_reduce(r_s[:, 4, :], r_a[:, :, :], AX_X, ALU.max))

            def router_second(b):
                link(dve.tensor_tensor(r_sel[:, b, 0, :, :], r_a[:, :, :], over_experts(r_s[:, 4, :]), ALU.is_equal))
                link(dve.scalar_tensor_tensor(r_a[:, :, :], r_sel[:, b, 0, :, :], -2.0, r_p[:, :, :],
                                              ALU.mult, ALU.add))
                link(dve.tensor_reduce(r_s[:, 3, :], r_a[:, :, :], AX_X, ALU.max))

            def router_weight(b):
                step(dve.tensor_tensor(r_a[:, :, :], r_a[:, :, :], over_experts(r_s[:, 3, :]), ALU.is_equal))
                link(dve.tensor_tensor(r_s[:, 6, :], r_s[:, 2, :], r_s[:, 3, :], ALU.add))
                step(dve.tensor_tensor(r_a[:, :, :], r_a[:, :, :], order, ALU.mult))
                link(dve.tensor_scalar(r_s[:, 6, :], r_s[:, 6, :], 1e-9, None, ALU.max))
                step(dve.tensor_reduce(r_s[:, 5, :], r_a[:, :, :], AX_X, ALU.max))
                link(dve.reciprocal(r_s[:, 7, :], r_s[:, 6, :]))
                step(dve.tensor_tensor(r_sel[:, b, 1, :, :], r_a[:, :, :], over_experts(r_s[:, 5, :]), ALU.is_equal))
                dve.wait_ge(dve_step, steps[0])
                dve.tensor_tensor(r_w[:, b, :, :], r_s[:, 2:4, :],
                                  r_s[:, 7, :].unsqueeze(1).broadcast_to([P, 2, TB]), ALU.mult)\
                   .then_inc(top2_done, 1)

            def hid_high(b):
                i = number(b)
                dve.wait_ge(square_done, i + 1)
                at_least(dve, down_done, i - BPN + 1)
                dve.tensor_copy(hid_hi[:, place(b), :], hid[:, b[2], :]).then_inc(hid_hi_done, 1)

            def hid_low(b):
                dve.wait_ge(hid_hi_done, number(b) + 1)
                dve.tensor_tensor(hid_lo[:, place(b), :], hid[:, b[2], :], hid_hi[:, place(b), :].bitcast(F32),
                                  ALU.subtract).then_inc(hid_lo_done, 1)

            def xs_high(m, h):
                if known(m) and m.n == 1:
                    dve.wait_ge(xs_first_done, h + 1)
                elif known(m) and m.n == 2:
                    dve.wait_ge(xs_second_done, h + 1)
                else:
                    dve.wait_ge(xs_done, 2 * (m.n - 3) + h + 1)
                if known(m) and m.n == 2:
                    dve.wait_ge(up_done, number((net(2 * h), 0, FT - 1)) + 1)
                elif known(m) and m.n == 3:
                    dve.wait_ge(up_done, number((net(1), h, FT - 1)) + 1)
                elif not known(m) or m.n > 3:
                    dve.wait_ge(up_done, number((preceding(m), h, FT - 1)) + 1)
                hi, _ = split_input(m, h)
                dve.tensor_copy(hi, xs[:, h, :]).then_inc(xs_hi_done, 1)

            def xs_low(m, h):
                hi, lo = split_input(m, h)
                dve.wait_ge(xs_hi_done, xs_number(m, h) + 1)
                dve.tensor_tensor(lo, xs[:, h, :], hi.bitcast(F32), ALU.subtract)\
                    .then_inc(xs_lo_done, 1)

            def split_xs(m, h):
                xs_high(m, h)
                xs_low(m, h)

            def scale_x_first(h):
                dve.wait_ge(spread_done, h + 1)
                dve.tensor_tensor(xs[:, h, :], xn2_t[:, h, :], ps[:, SPREAD_BANK[h], :], ALU.mult)\
                    .then_inc(xs_first_done, 1)
                split_xs(net(1), h)

            dve.wait_ge(const_ready, 1)
            router_sub(0)
            router_first(0)
            router_second(0)
            router_weight(0)
            residual(1)

            def hidden(b, prev):
                hid_high(b)
                if prev is not None and not on_pool(prev):
                    hid_low(prev)

            for i in range(EARLY):
                hidden(BLOCKS[i], BLOCKS[i - 1] if i else None)
                if i == 0:
                    scale_x_first(0)
                if i == 3:
                    layer_norm_stats(1, x2, 1)
                    scale_x(dve, net(2), 0)
                    xs_high(net(2), 0)
                    layer_norm_apply(3, 1, x2, xn2, 1)
                    xs_low(net(2), 0)
                if i == 5:
                    router_sub(1)
                if i == 6:
                    router_first(1)
                    router_second(1)
                if i == 7:
                    router_weight(1)
                if i == 12:
                    scale_x_first(1)
                if i == 16:
                    scale_x(dve, net(2), 1)
                    split_xs(net(2), 1)
                if i == 19:
                    split_xs(net(3), 0)
                if i == 23:
                    split_xs(net(3), 1)

            def network(m):
                for h in range(B):
                    for f in range(FT):
                        hidden((m, h, f), back((m, h, f), 1))
                        if f == FT - 1 and not (known(m) and m.n == NN - 1):
                            split_xs(following(m), h)

            run_networks(dve, network)
            for i in range(2 * B):
                tiles = slice(i * TB // 2, (i + 1) * TB // 2)
                dve.wait_ge(y_t_done, i + 1)
                dve.tensor_tensor(y_out[:, tiles, :],
                                  ps[:, OUT_BANK[i], 0:S // 2].rearrange("p (t d) -> p t d", d=D),
                                  x2[:, tiles, :], ALU.add).then_inc(y_ready, 1)

        @block.tensor
        def _(pe):
            def three(out_ap, w, wl, m, ml, start, stop):
                pe.matmul(out_ap, lhsT=w, rhs=m, start=start, stop=False)
                pe.matmul(out_ap, lhsT=w, rhs=ml, start=False, stop=False)
                return pe.matmul(out_ap, lhsT=wl, rhs=m, start=False, stop=stop)

            pe.wait_ge(warm_ready, 1)

            def keep_warm(count):
                for _ in range(count):
                    pe.matmul(ps[:, 3, :], lhsT=warm[:, 0:P], rhs=warm[:, :], start=True, stop=True)

            keep_warm(WARM)

            pe.wait_ge(bd_ready, 3)
            pe.wait_ge(ctx_in, 16)

            def bd_of(i):
                return bd[:, i, :, :].rearrange("p h e -> p (h e)")

            pe.matmul(ps[:, PROB_BANK[0], 0:B * SK], lhsT=bd_of(0), rhs=ctx_sb[:, :], start=True, stop=True)
            pe.matmul(ps[:, PROB_BANK[0], 256:256 + B * SK], lhsT=bd_of(2), rhs=ctx_sb[:, :],
                      start=True, stop=True).then_inc(kv_done, 1)
            pe.wait_ge(kv_read, 1)
            pe.matmul(ps[:, PROB_BANK[1], 0:B * SK], lhsT=bd_of(1), rhs=k_t[:, :],
                      start=True, stop=True).then_inc(kq_done, 1)

            def transpose_x(i, src, g, bank, done):
                for t in range(TB):
                    pe.wait_ge(xn_ready, TB * i + t + 1)
                    pe.transpose(ps[:, bank, t * P:(t + 1) * P], src[:, g * TB + t, :], ident[:, :])\
                        .then_inc(done, 1)

            pe.wait_ge(ident_ready, 1)
            for t in range(TB):
                pe.wait_ge(xn_ready, t + 1)
                if X_BANK[t] == PROB_BANK[0]:
                    pe.wait_ge(kv_read, 2)
                if X_BANK[t] == PROB_BANK[1]:
                    pe.wait_ge(kq_split, 2)
                pe.transpose(ps[:, X_BANK[t], 0:P], xn[:, t, :], ident[:, :]).then_inc(xt_done, 1)
                keep_warm(1 if t < TB - 1 else 3)
            pe.wait_ge(ident_ready, 2)
            pe.wait_ge(bias_ready, 1)

            def scores(k):
                b, half, qt = k // UPB, k % UPB // TB, k % TB
                if k < TB:
                    pe.wait_ge(xn_lo_done, k + 1)
                if qt == 0:
                    pe.wait_ge(kblk_ready[b][half], 2)
                if k == 1:
                    pe.wait_ge(bias_ready, 2)
                if k == UPB:
                    pe.wait_ge(bias_ready, 3)
                if k == UPB:
                    pe.wait_ge(xn_lo_done, TB + 1)
                at_least(pe, sub_done, k - 1)
                for i in range(2):
                    g = 2 * half + i
                    dst = heads_of(2 * (k % 2) + i)
                    q = slice(qt * P, (qt + 1) * P)
                    pe.matmul(dst, lhsT=ident_bf[:, :],
                              rhs=mask_bias[:, b * TB + qt, :].unsqueeze(1).broadcast_to([P, JH, SK]),
                              start=True, stop=False)
                    heads = slice(g * JH, (g + 1) * JH)
                    last = three(dst, xn_hi[:, b, q], xn_lo[:, b, q],
                                 kblk_hi[:, b, heads, :], kblk_lo[:, b, heads, :], False, True)
                last.then_inc(score_done, 1)

            def transpose_probs(k):
                pe.wait_ge(norm_done, k + 1)
                pe.wait_ge(const_ready, 3)
                at_least(pe, pt_read, 2 * k)
                rows = prob_n[:, k % PNR, :, :].rearrange("p h k -> p (h k)")
                for c in range(CH):
                    i, at = (0, c) if c < 3 else (1, c - 3)
                    ins = pe.transpose(ps[:, PROB_BANK[i], at * P:(at + 1) * P],
                                       rows[:, c * P:(c + 1) * P], ident[:, :])
                    if c in (2, CH - 1):
                        ins.then_inc(pt_done, 1)

            def pv(b, c):
                half = c // CH
                if c % CH == 0:
                    pe.wait_ge(pt_read, 2 * (UPB * b + TB * (half + 1)))
                    if b > 0 and c == 0:
                        pe.wait_ge(attn_read, b)
                pe.wait_ge(vblk_ready, (b * 2 * CH + c) // 4 + 1)
                ins = pe.matmul(ps[:, PV_BANK, :], lhsT=vblk[:, b * 2 * CH + c, :],
                                rhs=prob_t[:, half, c % CH, :], start=(c == 0), stop=(c == 2 * CH - 1))
                if c % CH == CH - 1:
                    ins.then_inc(pv_done, 1)

            def project_out(b):
                pe.wait_ge(attn_read, b + 1)
                if b == 0:
                    pe.wait_ge(wo_in, 16)
                    pe.wait_ge(vblk_ready, 5)
                else:
                    pe.wait_ge(logit_read, b)
                for t in range(TB):
                    last = pe.matmul(ps[:, MISC_BANK, t * P:(t + 1) * P], lhsT=attn_t[:, t * P:(t + 1) * P],
                                     rhs=wo_sb[:, 0:D], start=True, stop=True)
                last.then_inc(proj_o, 1)

            pv_at = {7: (0, (0,)), 8: (0, (1,)), 9: (0, (2,)), 10: (0, (3,)),
                     11: (0, (4, 5)), 12: (0, (6,)), 13: (0, (7,)), 14: (0, (8, 9)),
                     15: (1, (0,)), 16: (1, (1, 2)), 17: (1, (3, 4))}
            for k in range(NU + TLAG):
                if k < NU:
                    scores(k)
                if k == 4:
                    transpose_x(1, xn, 1, PV_BANK, xt_done)
                if k >= TLAG:
                    transpose_probs(k - TLAG)
                if 4 <= k < 9:
                    r = k - 4
                    if r == 0:
                        pe.wait_ge(xn_lo_done, TB)
                        pe.wait_ge(vblk_t_ready, 1)
                    if r == 2:
                        pe.wait_ge(vblk_t_ready, 2)
                    at_least(pe, vblk_ready, r)
                    pe.wait_ge(const_ready, 2)
                    flat = vblk_t[:, :, :, :].rearrange("p b h k -> p (b h k)")
                    for j in range(4):
                        c = 4 * r + j
                        last = pe.transpose(ps[:, MISC_BANK, j * P:(j + 1) * P], flat[:, c * P:(c + 1) * P],
                                            ident[:, :])
                    last.then_inc(vt_done, 1)
                if k == 15:
                    project_out(0)
                if k in pv_at:
                    b, chunks = pv_at[k]
                    if k == 7:
                        pe.wait_ge(xn_lo_done, TB + 1)
                    for c in chunks:
                        pv(b, c)
                if k == 17:
                    pe.wait_ge(x2_done, 1)
                    transpose_x(2, xn2, 0, MISC_BANK, xt2_done)

            def logits(b):
                pe.wait_ge(xn2_read, b + 1)
                if b == 1:
                    pe.wait_ge(root_t_read, 1)
                for t in range(TB):
                    last = pe.matmul(ps[:, LOGIT_BANK[b], t * NE:(t + 1) * NE],
                                     lhsT=xn2_t[:, b, t * P:(t + 1) * P],
                                     rhs=wo_sb[:, D:D + NE], start=True, stop=True)
                last.then_inc(logit_done, 1)

            def transpose_root(b):
                pe.wait_ge(root_done, b + 1)
                if b == 0:
                    pe.wait_ge(attn_read, 2)
                else:
                    pe.wait_ge(xn2_read, 2)
                pe.transpose(ps[0:TB * NE, ROOT_BANK[b], 0:P], root[:, b, :, :].rearrange("p t e -> p (t e)"),
                             ident[:, :]).then_inc(root_t_done, 1)

            def spread_root(b):
                if b == 0:
                    pe.wait_ge(pt_read, 2 * NU)
                else:
                    pe.wait_ge(logit_read, 2)
                pe.wait_ge(root_done, b + 1)
                for t in range(TB):
                    last = pe.transpose(ps[:, SPREAD_BANK[b], t * P:(t + 1) * P],
                                        root[:, b, t, 0:1].broadcast_to([P, P]), ident[:, :])
                last.then_inc(spread_done, 1)

            def up(b):
                m, h, f = b
                i = number(b)
                first = known(m) and m.n == 0
                if isinstance(i, int) and i < FT:
                    pe.wait_ge(sub_done, NU - 1 + f // 2)
                at_least(pe, relu_done, i - FT + 1)
                w_h, w_l = split_weights(m)
                if h == 0 and f == 0:
                    pe.wait_ge(w_lo_done[UP], m.n + 1)
                if f == 0:
                    if first:
                        pe.wait_ge(x2_lo_done, h + 1)
                    else:
                        pe.wait_ge(xs_lo_done, xs_number(m, h) + 1)
                hi, lo = split_input(m, h)
                w = slice(f * P, (f + 1) * P)
                three(ps[:, f, :], w_h[:, w], w_l[:, w], hi, lo, True, True)\
                    .then_inc(up_done, 1)

            def down(b):
                m, h, f = b
                at = place(b)
                w_h, w_l = split_weights(m)
                if known(m) and m.n == 0 and f == 0:
                    if h == 0:
                        pe.wait_ge(pt_read, 2 * NU)
                    else:
                        pe.wait_ge(xs_first_done, 1)
                if h == 0 and f == 0:
                    pe.wait_ge(w_lo_done[DOWN], m.n + 1)
                wait_low(pe, b)
                w = slice(FF + f * P, FF + (f + 1) * P)
                three(ps[:, Y_BANK[h], :], w_h[:, w], w_l[:, w], hid_hi[:, at, :], hid_lo[:, at, :],
                      known(m) and m.n == 0 and f == 0, known(m) and m.n == NN - 1 and f == FT - 1)\
                    .then_inc(down_done, 1)

            logits(0)
            for c in range(CH, 2 * CH):
                pv(1, c)
            downs_after = {3: (0,), 4: (1,), 5: (2,), 7: (3,), 10: (4,), 11: (5,), 12: (6,), 13: (7,), 14: (8,),
                           15: (9, 10, 11), 18: (12,), 19: (13, 14, 15), 22: (16,), 23: (17,)}
            for i in range(EARLY):
                up(BLOCKS[i])
                if i == 1:
                    project_out(1)
                if i == 2:
                    transpose_root(0)
                    spread_root(0)
                if i == 7:
                    pe.wait_ge(x2_done, 2)
                    transpose_x(3, xn2, 1, MISC_BANK, xt2_done)
                for j in downs_after.get(i, ()):
                    down(BLOCKS[j])
                if i == 8:
                    logits(1)
                if i == 14:
                    transpose_root(1)
                    spread_root(1)

            def network(m):
                for h in range(B):
                    for f in range(FT):
                        up((m, h, f))
                        down(back((m, h, f), LAG))

            run_networks(pe, network)
            for b in BLOCKS[NB - LAG:]:
                down(b)
            for i in range(2 * B):
                pe.wait_ge(y_read, i + 1)
                at_least(pe, y_ready, i - 1)
                for t in range(TB // 2):
                    at = (i % 2 * TB // 2 + t) * P
                    last = pe.transpose(ps[:, OUT_BANK[i], t * P:(t + 1) * P], y_t[:, i // 2, at:at + P],
                                        ident[:, :])
                last.then_inc(y_t_done, 1)


def kernel(x, ctx_1024, mask_Bx1xSxS2_ik1, L0_xattn_Wv, L0_xattn_Wk, L0_xattn_Wq, L0_xattn_Wo, L0_xattn_bo,
           L0_ffn_router_w, L0_ffn_w_fc, L0_ffn_w_proj, L0_ffn_shared_fc, L0_ffn_shared_proj):
    import numpy as np
    import concourse.bacc as bacc
    from concourse.bass_utils import run_bass_kernel_spmd

    up = np.concatenate([np.asarray(L0_ffn_shared_fc)[None], np.asarray(L0_ffn_w_fc)]).transpose(0, 2, 1)
    down = np.concatenate([np.asarray(L0_ffn_shared_proj)[None], np.asarray(L0_ffn_w_proj)])
    down = down.reshape(NN, D, FT, P).transpose(0, 3, 2, 1).reshape(NN, P, FF)
    arrays = {
        "x": np.asarray(x).reshape(B * S, D),
        "ctx_t": np.asarray(ctx_1024).transpose(2, 0, 1).reshape(D, B * SK),
        "mask": np.asarray(mask_Bx1xSxS2_ik1).reshape(B * S, SK),
        "small": np.concatenate([np.asarray(L0_xattn_Wk).T, np.asarray(L0_xattn_Wq), np.asarray(L0_xattn_Wv).T],
                                axis=1),
        "wo_r": np.concatenate([np.asarray(L0_xattn_Wo).T, np.asarray(L0_ffn_router_w).T], axis=1),
        "bo": np.asarray(L0_xattn_bo),
        "w_all": np.concatenate([up, down], axis=2),
    }
    nc = bacc.Bacc("TRN2", target_bir_lowering=False, num_devices=1)
    args = []
    for name, a in arrays.items():
        arrays[name] = a = np.ascontiguousarray(a)
        args.append(nc.dram_tensor(name, a.shape, mybir.dt.from_np(a.dtype), kind="ExternalInput").ap())
    args.append(nc.dram_tensor("out", (B * S, D), F32, kind="ExternalOutput").ap())
    xattn_moe(nc, *args)
    r = run_bass_kernel_spmd(nc, [arrays], core_ids=[0])
    return r.results[0]["out"].reshape(B, S, D)
```
